# Optimizing a Trainium2 kernel written in Bass

```python
import numpy as np
import jax
import jax.numpy as jnp

def _softmax(x, axis=-1):
    return jax.nn.softmax(x, axis=axis)

def _gelu(x):
    return jax.nn.gelu(x, approximate=True)

def _silu(x):
    return jax.nn.silu(x)

def _sigmoid(x):
    return jax.nn.sigmoid(x)

def _layernorm(x, axis=-1, eps=1e-05):
    m = jnp.mean(x, axis=axis, keepdims=True)
    v = jnp.var(x, axis=axis, keepdims=True)
    return (x - m) / jnp.sqrt(v + eps)

def _scatter_add(tgt, idx, src, axis=0):
    return tgt.at[idx].add(src)

def _segment_sum(src, seg, n):
    return jax.ops.segment_sum(src, seg, n)
kernel_name = 'mk_gnn_preln_d4_gnn_r32_7e534f'

def setup_inputs(seed: int=0):
    np.random.seed(seed)
    _w = jnp.asarray

    def _rec_inputs():
        import jax
        import jax.numpy as jnp
        _gk = jax.random.key(seed)
        x = -0.000202 + 1 * jax.random.normal(jax.random.fold_in(_gk, 1), (3125, 128), jnp.float32)
        src = jax.random.randint(jax.random.fold_in(_gk, 2), (50000,), 0, 3125, jnp.int32)
        dst = jnp.minimum((3125 * jax.random.uniform(jax.random.fold_in(_gk, 3), (50000,)) ** 2.0).astype(jnp.int32), 99999)
        _o = jnp.argsort(dst, stable=True)
        src = src[_o]
        dst = dst[_o]
        edge_attr_32 = 0.000196303 + 1.00016 * jax.random.normal(jax.random.fold_in(_gk, 11), (50000, 32), jnp.float32)
        edge_attr_64 = 0.000189758 + 1.00013 * jax.random.normal(jax.random.fold_in(_gk, 12), (50000, 64), jnp.float32)
        edge_type_5 = jax.random.randint(jax.random.fold_in(_gk, 14), (50000,), 0, 5, jnp.int32)
        node_type_3 = jax.random.randint(jax.random.fold_in(_gk, 15), (3125,), 0, 3, jnp.int32)
        return (x, src, dst, edge_attr_32, edge_attr_64, edge_type_5, node_type_3)
    x, src, dst, edge_attr_32, edge_attr_64, edge_type_5, node_type_3 = _rec_inputs()

    def _L0_gnn_setup():
        import jax, jax.numpy as jnp
        import numpy as np
        N, E, IN_DIM, EDGE_DIM, HID, L = (50000, 25000, 128, 64, 128, 3)
        LN_EPS = 1e-05

        def _layer_norm(h, g, b):
            mu = h.mean(-1, keepdims=True)
            var = ((h - mu) ** 2).mean(-1, keepdims=True)
            return (h - mu) * jax.lax.rsqrt(var + LN_EPS) * g + b
        key = jax.random.key(seed)
        ks = jax.random.split(key, 12)
        s = 0.05
        return {'x': jax.random.normal(ks[0], (N, IN_DIM), dtype=jnp.float32), 'edge_index': jax.random.randint(ks[1], (2, E), 0, N, dtype=jnp.int64), 'edge_attr': jax.random.normal(ks[2], (E, EDGE_DIM), dtype=jnp.float32), 'We': jax.random.normal(ks[3], (L, EDGE_DIM, HID), dtype=jnp.float32) * s, 'be': jnp.zeros((L, HID), dtype=jnp.float32), 'W1': jax.random.normal(ks[4], (L, HID, HID), dtype=jnp.float32) * s, 'b1': jnp.zeros((L, HID), dtype=jnp.float32), 'W2': jax.random.normal(ks[5], (L, HID, HID), dtype=jnp.float32) * s, 'b2': jnp.zeros((L, HID), dtype=jnp.float32), 'gamma': jnp.ones((L, HID), dtype=jnp.float32), 'beta': jnp.zeros((L, HID), dtype=jnp.float32)}
    _L0_gnn_all = _L0_gnn_setup()
    _L0_gnn_in = {k: v for k, v in _L0_gnn_all.items() if k in ('We', 'be', 'W1', 'b1', 'W2', 'b2', 'gamma', 'beta')}
    del _L0_gnn_all

    def _L1_gnn_setup():
        import jax, jax.numpy as jnp
        import numpy as np
        N_NODES = 50000
        N_EDGES = 25000
        IN_DIM = 128
        OUT_DIM = 128
        N_REL = 5
        ALPHA = 0.2
        NEG_INF = -1e+30

        def _rgat_forward(node_features, edge_index, edge_type, WQ, WK, WV, a_vec):
            num_nodes = node_features.shape[0]
            out_dim = WQ.shape[-1]
            src = edge_index[0]
            tgt = edge_index[1]
            a_q = a_vec[:out_dim]
            a_k = a_vec[out_dim:]
            h_prime = jnp.zeros((num_nodes, out_dim), dtype=node_features.dtype)
            for r in range(WQ.shape[0]):
                Qn = node_features @ WQ[r]
                Kn = node_features @ WK[r]
                Vn = node_features @ WV[r]
                e = Qn[tgt] @ a_q + Kn[src] @ a_k
                e = jnp.where(e >= 0, e, ALPHA * e)
                mask = edge_type == r
                e_m = jnp.where(mask, e, NEG_INF)
                e_max = jax.ops.segment_max(e_m, tgt, num_segments=num_nodes)
                e_exp = jnp.exp(e_m - e_max[tgt])
                e_sum = jax.ops.segment_sum(e_exp, tgt, num_segments=num_nodes)
                attn = e_exp / (e_sum[tgt] + 1e-10)
                weighted = jnp.where(mask[:, None], Vn[src] * attn[:, None], 0.0)
                h_prime = h_prime + jax.ops.segment_sum(weighted, tgt, num_segments=num_nodes)
            return jax.nn.elu(h_prime)
        key = jax.random.key(seed)
        ks = jax.random.split(key, 7)
        node_features = jax.random.normal(ks[0], (N_NODES, IN_DIM), dtype=jnp.float32)
        edge_index = jax.random.randint(ks[1], (2, N_EDGES), 0, N_NODES, dtype=jnp.int32)
        edge_type = jax.random.randint(ks[2], (N_EDGES,), 0, N_REL, dtype=jnp.int32)
        lim = float(np.sqrt(6.0 / (IN_DIM + OUT_DIM))) * 1.414
        WQ = jax.random.uniform(ks[3], (N_REL, IN_DIM, OUT_DIM), jnp.float32, -lim, lim)
        WK = jax.random.uniform(ks[4], (N_REL, IN_DIM, OUT_DIM), jnp.float32, -lim, lim)
        WV = jax.random.uniform(ks[5], (N_REL, IN_DIM, OUT_DIM), jnp.float32, -lim, lim)
        lim_a = float(np.sqrt(6.0 / (2 * OUT_DIM + 1))) * 1.414
        a_vec = jax.random.uniform(ks[6], (2 * OUT_DIM,), jnp.float32, -lim_a, lim_a)
        return {'node_features': node_features, 'edge_index': edge_index, 'edge_type': edge_type, 'WQ': WQ, 'WK': WK, 'WV': WV, 'a_vec': a_vec}
    _L1_gnn_all = _L1_gnn_setup()
    _L1_gnn_in = {k: v for k, v in _L1_gnn_all.items() if k in ('WQ', 'WK', 'WV', 'a_vec')}
    del _L1_gnn_all

    def _L2_gnn_setup():
        import jax, jax.numpy as jnp
        import numpy as np
        N_NODES = 50000
        N_EDGES = 25000
        D = 128
        H = 8
        HD = D // H
        N_NTYPES = 3
        N_ETYPES = 5
        LN_EPS = 1e-05

        def _layer_norm(y, g, b):
            m = y.mean(-1, keepdims=True)
            v = ((y - m) ** 2).mean(-1, keepdims=True)
            return (y - m) * jax.lax.rsqrt(v + LN_EPS) * g + b
        key = jax.random.key(seed)
        ks = jax.random.split(key, 16)
        inp = {'x': jax.random.normal(ks[0], (N_NODES, D), dtype=jnp.float32), 'edge_index': jax.random.randint(ks[1], (2, N_EDGES), 0, N_NODES), 'edge_type': jax.random.randint(ks[2], (N_EDGES,), 0, N_ETYPES), 'node_type': jax.random.randint(ks[3], (N_NODES,), 0, N_NTYPES), 'W_Q': jax.random.normal(ks[4], (N_NTYPES, H, HD, HD), dtype=jnp.float32) * 0.02, 'W_K': jax.random.normal(ks[5], (N_NTYPES, H, HD, HD), dtype=jnp.float32) * 0.02, 'W_V': jax.random.normal(ks[6], (N_NTYPES, H, HD, HD), dtype=jnp.float32) * 0.02, 'W_edge': jax.random.normal(ks[7], (N_ETYPES, H, HD, HD), dtype=jnp.float32) * 0.02, 'mu': jnp.ones((H, N_ETYPES), dtype=jnp.float32), 'W_out': jax.random.normal(ks[8], (D, D), dtype=jnp.float32) * 0.02, 'b_out': jnp.zeros((D,), dtype=jnp.float32), 'ln1_g': jnp.ones((D,), dtype=jnp.float32), 'ln1_b': jnp.zeros((D,), dtype=jnp.float32), 'W1': jax.random.normal(ks[9], (D, 4 * D), dtype=jnp.float32) * 0.02, 'b1': jnp.zeros((4 * D,), dtype=jnp.float32), 'W2': jax.random.normal(ks[10], (4 * D, D), dtype=jnp.float32) * 0.02, 'b2': jnp.zeros((D,), dtype=jnp.float32), 'ln2_g': jnp.ones((D,), dtype=jnp.float32), 'ln2_b': jnp.zeros((D,), dtype=jnp.float32)}
        return inp
    _L2_gnn_all = _L2_gnn_setup()
    _L2_gnn_in = {k: v for k, v in _L2_gnn_all.items() if k in ('W_Q', 'W_K', 'W_V', 'W_edge', 'mu', 'W_out', 'b_out', 'ln1_g', 'ln1_b', 'W1', 'b1', 'W2', 'b2', 'ln2_g', 'ln2_b')}
    del _L2_gnn_all

    def _L3_gnn_setup():
        import jax, jax.numpy as jnp
        import numpy as np
        N, E = (50000, 25000)
        NODE_DIM, EDGE_DIM, HIDDEN_DIM = (128, 32, 128)
        LN_EPS = 1e-05
        key = jax.random.key(seed)
        ks = jax.random.split(key, 10)

        def lin(k, fan_in, fan_out):
            bound = 1.0 / np.sqrt(fan_in)
            kw, kb = jax.random.split(k)
            W = jax.random.uniform(kw, (fan_out, fan_in), jnp.float32, -bound, bound)
            b = jax.random.uniform(kb, (fan_out,), jnp.float32, -bound, bound)
            return (W, b)
        x = jax.random.normal(ks[0], (N, NODE_DIM), jnp.float32)
        edge_index = jax.random.randint(ks[1], (2, E), 0, N, jnp.int64)
        edge_attr = jax.random.normal(ks[2], (E, EDGE_DIM), jnp.float32)
        W1, b1 = lin(ks[3], 2 * NODE_DIM + EDGE_DIM, HIDDEN_DIM)
        W2, b2 = lin(ks[4], HIDDEN_DIM, HIDDEN_DIM)
        Wu, bu = lin(ks[5], HIDDEN_DIM, NODE_DIM)
        gamma = jnp.ones((NODE_DIM,), jnp.float32)
        beta = jnp.zeros((NODE_DIM,), jnp.float32)
        return {'x': x, 'edge_attr': edge_attr, 'W1': W1, 'b1': b1, 'W2': W2, 'b2': b2, 'Wu': Wu, 'bu': bu, 'gamma': gamma, 'beta': beta, 'edge_index': edge_index}
    _L3_gnn_all = _L3_gnn_setup()
    _L3_gnn_in = {k: v for k, v in _L3_gnn_all.items() if k in ('W1', 'b1', 'W2', 'b2', 'Wu', 'bu', 'gamma', 'beta')}
    del _L3_gnn_all
    return {'x': x, 'src': src, 'dst': dst, 'edge_attr_32': edge_attr_32, 'edge_attr_64': edge_attr_64, 'edge_type_5': edge_type_5, 'node_type_3': node_type_3, 'L0_gnn_We': _L0_gnn_in['We'], 'L0_gnn_be': _L0_gnn_in['be'], 'L0_gnn_W1': _L0_gnn_in['W1'], 'L0_gnn_b1': _L0_gnn_in['b1'], 'L0_gnn_W2': _L0_gnn_in['W2'], 'L0_gnn_b2': _L0_gnn_in['b2'], 'L0_gnn_gamma': _L0_gnn_in['gamma'], 'L0_gnn_beta': _L0_gnn_in['beta'], 'L1_gnn_WQ': _L1_gnn_in['WQ'], 'L1_gnn_WK': _L1_gnn_in['WK'], 'L1_gnn_WV': _L1_gnn_in['WV'], 'L1_gnn_a_vec': _L1_gnn_in['a_vec'], 'L2_gnn_W_Q': _L2_gnn_in['W_Q'], 'L2_gnn_W_K': _L2_gnn_in['W_K'], 'L2_gnn_W_V': _L2_gnn_in['W_V'], 'L2_gnn_W_edge': _L2_gnn_in['W_edge'], 'L2_gnn_mu': _L2_gnn_in['mu'], 'L2_gnn_W_out': _L2_gnn_in['W_out'], 'L2_gnn_b_out': _L2_gnn_in['b_out'], 'L2_gnn_ln1_g': _L2_gnn_in['ln1_g'], 'L2_gnn_ln1_b': _L2_gnn_in['ln1_b'], 'L2_gnn_W1': _L2_gnn_in['W1'], 'L2_gnn_b1': _L2_gnn_in['b1'], 'L2_gnn_W2': _L2_gnn_in['W2'], 'L2_gnn_b2': _L2_gnn_in['b2'], 'L2_gnn_ln2_g': _L2_gnn_in['ln2_g'], 'L2_gnn_ln2_b': _L2_gnn_in['ln2_b'], 'L3_gnn_W1': _L3_gnn_in['W1'], 'L3_gnn_b1': _L3_gnn_in['b1'], 'L3_gnn_W2': _L3_gnn_in['W2'], 'L3_gnn_b2': _L3_gnn_in['b2'], 'L3_gnn_Wu': _L3_gnn_in['Wu'], 'L3_gnn_bu': _L3_gnn_in['bu'], 'L3_gnn_gamma': _L3_gnn_in['gamma'], 'L3_gnn_beta': _L3_gnn_in['beta']}

def reference(x, src, dst, edge_attr_32, edge_attr_64, edge_type_5, node_type_3, L0_gnn_We, L0_gnn_be, L0_gnn_W1, L0_gnn_b1, L0_gnn_W2, L0_gnn_b2, L0_gnn_gamma, L0_gnn_beta, L1_gnn_WQ, L1_gnn_WK, L1_gnn_WV, L1_gnn_a_vec, L2_gnn_W_Q, L2_gnn_W_K, L2_gnn_W_V, L2_gnn_W_edge, L2_gnn_mu, L2_gnn_W_out, L2_gnn_b_out, L2_gnn_ln1_g, L2_gnn_ln1_b, L2_gnn_W1, L2_gnn_b1, L2_gnn_W2, L2_gnn_b2, L2_gnn_ln2_g, L2_gnn_ln2_b, L3_gnn_W1, L3_gnn_b1, L3_gnn_W2, L3_gnn_b2, L3_gnn_Wu, L3_gnn_bu, L3_gnn_gamma, L3_gnn_beta):
    import jax
    import jax.numpy as jnp

    def _L0_gnn_ref(x, edge_index, edge_attr, We, be, W1, b1, W2, b2, gamma, beta):
        import jax, jax.numpy as jnp
        import numpy as np
        N, E, IN_DIM, EDGE_DIM, HID, L = (50000, 25000, 128, 64, 128, 3)
        LN_EPS = 1e-05

        def _layer_norm(h, g, b):
            mu = h.mean(-1, keepdims=True)
            var = ((h - mu) ** 2).mean(-1, keepdims=True)
            return (h - mu) * jax.lax.rsqrt(var + LN_EPS) * g + b
        src, dst = (edge_index[0], edge_index[1])
        n = x.shape[0]
        for l in range(L):
            e = edge_attr @ We[l] + be[l]
            m = jax.nn.relu(x[src] + e)
            agg = jax.ops.segment_sum(m, dst, num_segments=n)
            h = x + agg
            h = jax.nn.relu(h @ W1[l] + b1[l]) @ W2[l] + b2[l]
            x = _layer_norm(jax.nn.relu(h), gamma[l], beta[l])
        return x

    def _L1_gnn_ref(node_features, edge_index, edge_type, WQ, WK, WV, a_vec):
        import jax, jax.numpy as jnp
        import numpy as np
        N_NODES = 50000
        N_EDGES = 25000
        IN_DIM = 128
        OUT_DIM = 128
        N_REL = 5
        ALPHA = 0.2
        NEG_INF = -1e+30

        def _rgat_forward(node_features, edge_index, edge_type, WQ, WK, WV, a_vec):
            num_nodes = node_features.shape[0]
            out_dim = WQ.shape[-1]
            src = edge_index[0]
            tgt = edge_index[1]
            a_q = a_vec[:out_dim]
            a_k = a_vec[out_dim:]
            h_prime = jnp.zeros((num_nodes, out_dim), dtype=node_features.dtype)
            for r in range(WQ.shape[0]):
                Qn = node_features @ WQ[r]
                Kn = node_features @ WK[r]
                Vn = node_features @ WV[r]
                e = Qn[tgt] @ a_q + Kn[src] @ a_k
                e = jnp.where(e >= 0, e, ALPHA * e)
                mask = edge_type == r
                e_m = jnp.where(mask, e, NEG_INF)
                e_max = jax.ops.segment_max(e_m, tgt, num_segments=num_nodes)
                e_exp = jnp.exp(e_m - e_max[tgt])
                e_sum = jax.ops.segment_sum(e_exp, tgt, num_segments=num_nodes)
                attn = e_exp / (e_sum[tgt] + 1e-10)
                weighted = jnp.where(mask[:, None], Vn[src] * attn[:, None], 0.0)
                h_prime = h_prime + jax.ops.segment_sum(weighted, tgt, num_segments=num_nodes)
            return jax.nn.elu(h_prime)
        return _rgat_forward(node_features, edge_index, edge_type, WQ, WK, WV, a_vec)

    def _L2_gnn_ref(x, edge_index, edge_type, node_type, W_Q, W_K, W_V, W_edge, mu, W_out, b_out, ln1_g, ln1_b, W1, b1, W2, b2, ln2_g, ln2_b):
        import jax, jax.numpy as jnp
        import numpy as np
        N_NODES = 50000
        N_EDGES = 25000
        D = 128
        H = 8
        HD = D // H
        N_NTYPES = 3
        N_ETYPES = 5
        LN_EPS = 1e-05

        def _layer_norm(y, g, b):
            m = y.mean(-1, keepdims=True)
            v = ((y - m) ** 2).mean(-1, keepdims=True)
            return (y - m) * jax.lax.rsqrt(v + LN_EPS) * g + b
        N = x.shape[0]
        xh = x.reshape(N, H, HD)
        Q = jnp.zeros_like(xh)
        K = jnp.zeros_like(xh)
        V = jnp.zeros_like(xh)
        for t in range(N_NTYPES):
            m = (node_type == t)[:, None, None]
            Q = jnp.where(m, jnp.einsum('nhd,hdf->nhf', xh, W_Q[t]), Q)
            K = jnp.where(m, jnp.einsum('nhd,hdf->nhf', xh, W_K[t]), K)
            V = jnp.where(m, jnp.einsum('nhd,hdf->nhf', xh, W_V[t]), V)
        src, dst = (edge_index[0], edge_index[1])
        q_dst = Q[dst]
        k_src = K[src]
        kt = jnp.zeros_like(k_src)
        for et in range(N_ETYPES):
            m = (edge_type == et)[:, None, None]
            kt = jnp.where(m, jnp.einsum('ehd,hdf->ehf', k_src, W_edge[et]), kt)
        scores = (q_dst * kt).sum(-1) / jnp.sqrt(jnp.float32(HD))
        scores = scores * mu[:, edge_type].T
        smax = jax.ops.segment_max(scores, dst, num_segments=N)
        ex = jnp.exp(scores - smax[dst])
        den = jax.ops.segment_sum(ex, dst, num_segments=N)
        w = ex / (den[dst] + 1e-10)
        agg = jax.ops.segment_sum(V[src] * w[..., None], dst, num_segments=N)
        mh = agg.reshape(N, D) @ W_out + b_out
        h = _layer_norm(x + mh, ln1_g, ln1_b)
        ffn = jax.nn.gelu(h @ W1 + b1, approximate=False) @ W2 + b2
        return _layer_norm(h + ffn, ln2_g, ln2_b)

    def _L3_gnn_ref(x, edge_attr, W1, b1, W2, b2, Wu, bu, gamma, beta, edge_index):
        import jax, jax.numpy as jnp
        import numpy as np
        N, E = (50000, 25000)
        NODE_DIM, EDGE_DIM, HIDDEN_DIM = (128, 32, 128)
        LN_EPS = 1e-05
        src, dst = (edge_index[0], edge_index[1])
        msg_input = jnp.concatenate([x[src], x[dst], edge_attr], axis=-1)
        h = jax.nn.relu(msg_input @ W1.T + b1)
        messages = h @ W2.T + b2
        agg = jax.ops.segment_sum(messages, dst, num_segments=x.shape[0])
        upd = jax.nn.relu(agg @ Wu.T + bu)
        y = x + upd
        mean = jnp.mean(y, axis=-1, keepdims=True)
        var = jnp.mean(jnp.square(y - mean), axis=-1, keepdims=True)
        return (y - mean) * jax.lax.rsqrt(var + LN_EPS) * gamma + beta
    edge_index = jnp.stack([src, dst])
    h = jnp.maximum(_layernorm(x, axis=-1), 0.0)
    x = x + _L0_gnn_ref(h, edge_index, edge_attr_64, L0_gnn_We, L0_gnn_be, L0_gnn_W1, L0_gnn_b1, L0_gnn_W2, L0_gnn_b2, L0_gnn_gamma, L0_gnn_beta)
    h = jnp.maximum(_layernorm(x, axis=-1), 0.0)
    x = x + _L1_gnn_ref(h, edge_index, edge_type_5, L1_gnn_WQ, L1_gnn_WK, L1_gnn_WV, L1_gnn_a_vec)
    h = jnp.maximum(_layernorm(x, axis=-1), 0.0)
    x = x + _L2_gnn_ref(h, edge_index, edge_type_5, node_type_3, L2_gnn_W_Q, L2_gnn_W_K, L2_gnn_W_V, L2_gnn_W_edge, L2_gnn_mu, L2_gnn_W_out, L2_gnn_b_out, L2_gnn_ln1_g, L2_gnn_ln1_b, L2_gnn_W1, L2_gnn_b1, L2_gnn_W2, L2_gnn_b2, L2_gnn_ln2_g, L2_gnn_ln2_b)
    h = jnp.maximum(_layernorm(x, axis=-1), 0.0)
    x = x + _L3_gnn_ref(h, edge_attr_32, L3_gnn_W1, L3_gnn_b1, L3_gnn_W2, L3_gnn_b2, L3_gnn_Wu, L3_gnn_bu, L3_gnn_gamma, L3_gnn_beta, edge_index)
    return x

_drawn_inputs = setup_inputs


def setup_inputs(seed=0):
    import zlib

    import numpy as np

    out = dict(_drawn_inputs(seed))
    spreads = {'L0_gnn_be': (0.0, 0.1),
     'L0_gnn_b1': (0.0, 0.1),
     'L0_gnn_b2': (0.0, 0.1),
     'L0_gnn_gamma': (1.0, 0.2),
     'L0_gnn_beta': (0.0, 0.1),
     'L2_gnn_mu': (1.0, 0.6),
     'L2_gnn_b_out': (0.0, 0.269),
     'L2_gnn_ln1_g': (1.0, 0.2),
     'L2_gnn_ln1_b': (0.0, 0.329),
     'L2_gnn_b1': (0.0, 0.8),
     'L2_gnn_b2': (0.0, 0.306),
     'L2_gnn_ln2_g': (1.0, 0.2),
     'L2_gnn_ln2_b': (0.0, 0.281),
     'L3_gnn_gamma': (1.0, 0.2),
     'L3_gnn_beta': (0.0, 0.342)}
    factors = {'L2_gnn_W_Q': 8.0,
     'L2_gnn_W_K': 8.0,
     'L2_gnn_W_V': 8.0,
     'L2_gnn_W_edge': 8.0,
     'L2_gnn_W_out': 8.0,
     'L2_gnn_W1': 3.443,
     'L2_gnn_W2': 3.366,
     'L3_gnn_b1': 2.961,
     'L3_gnn_bu': 5.801}
    for name, (base, spread) in spreads.items():
        noise = np.random.default_rng([zlib.crc32(name.encode()), seed]).standard_normal(out[name].shape)
        drawn = base * np.exp(spread * noise) if base else spread * noise
        out[name] = jnp.asarray(drawn.astype(out[name].dtype))
    for name, factor in factors.items():
        out[name] = (out[name] * factor).astype(out[name].dtype)
    return out
```

```python
from contextlib import ExitStack

import numpy as np

import concourse.bass as bass
from concourse import mybir

F32 = mybir.dt.float32
I32 = mybir.dt.int32
ALU = mybir.AluOpType
ACT = mybir.ActivationFunctionType
DVE, PE = mybir.EngineType.DVE, mybir.EngineType.PE
AX = mybir.AxisListType.X

P = 128
N, E, D = 3125, 50000, 128
NBLK = (N + P - 1) // P
NPAD = NBLK * P
LASTROWS = N - (NBLK - 1) * P
EA, EB = 64, 32
NREL, NTYPE, NHEAD = 5, 3, 8
HD = D // NHEAD
FF = 4 * D
EP, EC = 125, 400
B = 4
NT = -(-((E + NBLK * (P - 1)) // P) // (2 * B)) * 2 * B
NB = NT // B
REC = EA + EB + 4
SC = 8
FILL = 13
G = 400
NG = NPAD // G
T1W = D + 4
EAB = EA + EB
W2N = D + NHEAD
LN_EPS = 1e-5
BIG = 1e30


def build(nc, a, out):
    ctx = ExitStack()
    with ctx:
        def sb(name, shape, dt=F32):
            return ctx.enter_context(nc.sbuf_tensor(name, shape, dt))

        def sem(name):
            return ctx.enter_context(nc.semaphore(name))

        def dram(name, shape, dt=F32):
            return nc.dram_tensor(name, shape, dt, kind="Internal").ap()

        rec = dram("slot_records", [NT * P, REC])
        eat = dram("edge_attr_T", [NB, EAB, B * P])
        tab0 = dram("table_gine", [NPAD, D])
        tab1 = dram("table_rel", [NPAD * NREL, T1W])
        tab2k = dram("table_keys", [NPAD * NREL, D])
        tab2v = dram("table_values", [NPAD, D])
        tab3 = dram("table_msg", [NPAD, D])

        ident = sb("ident", [P, P])
        iota_n = sb("iota_n", [P, P])
        ones = sb("ones", [P, P])
        tri = sb("tri", [P, P])
        dl = sb("dl", [P, NT])
        et = sb("et", [P, NT])
        idx1 = sb("idx1", [P, NT + B], I32)
        idx5 = sb("idx5", [P, NT + B], I32)
        nb = sb("nb", [P, NT], I32)
        score = sb("score", [P, NT * NHEAD])
        X = sb("X", [P, NBLK, D])
        H = sb("H", [P, NBLK, D])
        AG = sb("AG", [P, NBLK * W2N])
        MX = sb("MX", [P, NBLK, NHEAD])
        C1 = sb("C1", [P, NBLK, 2 * NREL])
        arena = sb("arena", [P, 5 * NPAD])
        ring = sb("ring", [P, 4, B, T1W])
        idxr = sb("idxr", [P, 4, B], I32)
        oh = sb("oh", [P, 4, B, P])
        ohT = sb("ohT", [P, 2, B, P])
        mraw = sb("mraw", [P, 2, B, P])
        msg = sb("msg", [P, 4, B, W2N])
        ear = sb("ear", [P, 2, B * P])
        small = sb("small", [P, 4, 64])
        small2 = sb("small2", [P, 4, 64])
        small3 = sb("small3", [P, 4, 64])
        small4 = sb("small4", [P, 4, 64])
        gm = sb("gm", [P, 4, B, 10])
        tz = sb("tz", [B * NHEAD, 2, 2 * P])
        ne = sb("ne", [B * NHEAD, 2, P + 1])
        sf = sb("sf", [B * NHEAD, 2, 2 * P])
        stat = sb("stat", [P, 4, 32])
        pcol = sb("pcol", [P, 2])
        wt = sb("wt", [P, 1300])
        bc = sb("bc", [P, 3, D])
        col = sb("col", [P, 16])
        b2row = sb("b2row", [1, D])

        ps = ctx.enter_context(nc.psum_tensor("ps", [P, 8, 512], F32))

        aren = arena[:, :]
        T = [aren[:, i * NPAD:(i + 1) * NPAD] for i in range(5)]


        slotr = sb("slotr", [P, 2, SC], I32)

        joined = sem("joined")
        dve_ch = sem("dve_chain")
        pn_full, pn_free = sem("node_psum_full"), sem("node_psum_free")
        ln_var, ln_std = sem("variance_ready"), sem("deviation_ready")
        w_in = sem("weights_in")
        t_out = sem("table_out")
        pool_go, act_go, pe_go = (sem(f"{e}_waits_passed") for e in ("pool", "act", "pe"))
        rows_rdy, vals_rdy = sem("rel_rows_ready"), sem("key_rows_ready")
        rows_out = [sem(f"rel_rows_out{h}") for h in range(2)]
        keys_out = [sem(f"key_rows_out{h}") for h in range(2)]
        rows_ch = sem("records_chain")
        rank_sem, sort2_sem, trs_sem = sem("places_chain"), sem("fields_chain"), sem("tr_score_chain")
        x_pad = sem("x_padding")
        relv_ps = sem("rel_vectors_in_psum")
        elu_in, elu_exp = sem("elu_input"), sem("elu_exp")
        kw_ps = sem("key_rows_in_psum")
        nt_ps, nt_free = sem("node_terms_in_psum"), sem("node_terms_taken")

        STAGES = (["slots", "records"]
                  + [f"{n}{l}" for l in range(3) for n in ("weights", "gine", "sumT", "hiddenT", "outT", "out", "norm")]
                  + ["rel_weights", "rel_T", "rel_vectors", "rel_table", "relA", "rel_max", "relD", "rel_den", "relB",
                     "rel_out"]
                  + ["tr_clear", "tr_weights", "tr_masked", "tr_T", "tr_keysT", "tr_qv", "tr_keys", "tr_values",
                     "trA", "tr_zero", "trB", "tr_mean", "tr_meanT", "tr_mixT", "tr_mix", "tr_norm1", "tr_norm1T",
                     "tr_hiddenT", "tr_ffT", "tr_ff", "tr_out"]
                  + ["mp_weights", "mp_T", "mp_node", "mp_table", "mp", "mp_sumT", "mp_msgT", "mp_updT", "mp_upd",
                     "mp_out"])

        class Join:
            def __init__(self, eng):
                self.eng, self.n = eng, 0

            def to(self, stage):
                upto = STAGES.index(stage) + 1
                assert upto > self.n, stage
                while self.n < upto:
                    self.n += 1
                    self.eng.drain()
                    self.eng.sem_inc(joined, 1)
                    self.eng.wait_ge(joined, 5 * self.n)

        class Chain:
            def __init__(self, eng, s):
                self.eng, self.s, self.n, self.base = eng, s, 0, 0

            def __call__(self, ins):
                self.n += 1
                ins.then_inc(self.s, 1)
                self.eng.wait_ge(self.s, self.base + self.n)

            def loop(self, start, stop, body, step=1):
                n0 = self.base + self.n
                self.base, self.n = n0, 0
                body(start)
                per = self.n
                with self.eng.Fori(start + step, stop, step) as i:
                    self.base, self.n = (i - start) * (per // step) + n0, 0
                    body(i)
                    assert self.n == per
                self.base, self.n = n0 + per * ((stop - start) // step), 0

        class Steps:
            def __init__(self, eng, s, per):
                self.eng, self.s, self.per, self.m = eng, s, per, per

            def start(self, n):
                assert self.m == self.per, (self.m, self.per)
                self.base, self.m = n * self.per, 0

            def __call__(self, ins):
                self.m += 1
                ins.then_inc(self.s, 1)
                self.eng.wait_ge(self.s, self.base + self.m)

        class Batch:
            def __init__(self, r, s, of=0):
                self.r, self.s, self.of = r, s, of
                self.k = r * 4 + s
                self.n = r * 4 + (s + of * NB)
                self.h, self.s4 = s % 2, s % 4
                self.i = r * 2 + (s // 2 + of * (NB // 2))
                self.u = r + (s // 4 + of * (NB // 4))

            def back(self, lag):
                return Batch(self.r, self.s - lag, self.of)

            def has(self, lag):
                return not isinstance(self.k, int) or self.k >= lag

            def real(self):
                return not isinstance(self.k, int) or 0 <= self.k < NB

            def late(self, lag):
                return not isinstance(self.n, int) or self.n >= lag

        def run(eng, stages, of=0):
            deep = max(lag for lag, _ in stages)
            lead = -(-deep // 4) + 1

            def turn(r, s):
                for lag, body in stages:
                    t = Batch(r, s, of).back(lag)
                    if t.real():
                        body(t)
            for k in range(4 * lead):
                turn(k // 4, k % 4)
            with eng.Fori(lead, NB // 4) as r:
                for s in range(4):
                    turn(r, s)
            for k in range(NB, NB + deep):
                turn(k // 4, k % 4)

        def halves(eng, body, n):
            for i in range(2):
                for h in range(2):
                    body(i, h, 2 * i + h)
            with eng.Fori(2, n // 2) as i:
                for h in range(2):
                    body(i, h, i * 2 + h)

        def late(k, n):
            return not isinstance(k, int) or k >= n

        def blocks_of(eng, which, t):
            _, values = nc.values_load_multi_w_load_instructions(
                nb[0:1, bass.ds(t.k * B, B)], engines=[which], min_val=0, max_val=NBLK - 1)
            return values

        class Sems:
            def __init__(self, p, *names, gath=False, ea=False):
                self.of = {n: sem(f"{p}_{n}") for n in names}
                self.gath = [sem(f"{p}_gathered{h}") for h in range(4)] if gath else None
                self.ea = [sem(f"{p}_attr_in{h}") for h in range(2)] if ea else None

            def __getitem__(self, name):
                return self.of[name]

        qg = Sems("gine", "index", "edge", "onehot", "added", "relu", "sums", "acc", gath=True, ea=True)
        qm = Sems("max", "index", "onehot", "turned", "onehotT", "node", "scores", "rows", "rows_sb", "scanned",
                  "back", "picked", "sums", "acc", "ch_score", "ch_scan", "ch_acc", gath=True)
        qd = Sems("relD", "onehot", "turned", "onehotT", "node", "logits", "exp", "weights", "sums", "acc", "chain",
                  "chain2")
        qr = Sems("relB", "index", "onehot", "turned", "onehotT", "node", "messages", "sums", "acc", "chain", gath=True)
        qt = Sems("trB", "index", "onehot", "turned", "onehotT", "node", "logits", "exp", "messages", "sums", "acc",
                  gath=True)
        qp = Sems("mp", "index", "onehot", "turned", "onehotT", "node", "added", "relu", "sums", "acc", gath=True, ea=True)
        qs = Sems("sort", "chain", "keys", "spread", "perm", "moved", "attr_sb", "fields")
        fill_out, cst, cst2 = sem("records_filled"), sem("constants"), sem("index_constants")
        el_in = sem("edge_list_in")
        cnt_rdy, cnt_ps = sem("counts_ready"), sem("counts_in_psum")
        att_in = [sem(f"attr_rows_in{h}") for h in range(2)]
        rec_rdy = sem("records_built")
        scat = [sem(f"records_scattered{h}") for h in range(2)]
        rin = [sem(f"records_in{h}") for h in range(4)]
        rout = [sem(f"attr_T_out{h}") for h in range(2)]
        fin = sem("result_out")

        cum = aren[0:EP, 0:NBLK * EC].rearrange("p (b c) -> p b c", b=NBLK)

        def spare(n, rows=EP):
            return aren[0:rows, NBLK * EC + n * EC:NBLK * EC + (n + 1) * EC]

        dsti, srci, eti, bki, slot = (spare(n).bitcast(I32) for n in (0, 1, 2, 3, 10))
        bkf, dstf, mask, zero, slotf, tmp = (spare(n) for n in (4, 5, 6, 7, 8, 9))
        fields = AG[0:EP, 0:4 * EC].rearrange("p (c f) -> p c f", f=4)
        iota_t, nbf = score[:, 0:NT], score[:, NT:2 * NT]
        recb = T[2][0:EP, 0:2 * SC * REC].rearrange("p (h c r) -> p h c r", h=2, c=SC)
        recin = T[3][:, 0:4 * B * REC].rearrange("p (h c r) -> p h c r", h=4, c=B)
        fillb = msg[:, :, :, :].rearrange("p a b d -> p (a b d)")[:, 0:FILL * REC].rearrange("p (s r) -> p s r", r=REC)
        keyT = T[4][:, 0:2 * B * P].rearrange("p (h b d) -> p h b d", h=2, b=B)
        perm = T[4][:, 2 * B * P:4 * B * P].rearrange("p (h b d) -> p h b d", h=2, b=B)
        eato = T[1][0:EAB, 0:2 * B * P].rearrange("p (h c) -> p h c", h=2)
        iota_p, iota_pi = pcol[:, 0:1], pcol[:, 1:2].bitcast(I32)
        cnt, prefix, tot, nt_f = (stat[:, q, 0:NBLK] for q in range(4))
        wend, wst, off = (small[:, 0, 0:NBLK], small[:, 1, 0:NBLK], small3[:, 0, 0:NBLK])
        nt_i = small2[:, 0, 0:NBLK].bitcast(I32)
        SK, PW = score[:, 0:NT], score[:, NT:2 * NT]
        XL = AG[:, 0:NPAD].rearrange("p (b d) -> p b d", b=NBLK)
        Qn = XL
        agg2 = AG[:, :].rearrange("p (b w) -> p b w", b=NBLK)
        agg3 = AG[:, 0:NBLK * (D + 1)].rearrange("p (b w) -> p b w", b=NBLK)
        DEN = MX[:, :, 0:NREL]
        T3 = [t.rearrange("p (b d) -> p b d", b=NBLK) for t in T]
        WK_o, WE = 768, score[:, 0:NREL * D]
        WQV = wt[:, 0:NTYPE * 2 * D].rearrange("p (t c) -> p t c", t=NTYPE)
        WKb = wt[:, WK_o:WK_o + NTYPE * D].rearrange("p (t c) -> p t c", t=NTYPE)
        WEb = WE.rearrange("p (t c) -> p t c", t=NREL)
        ntype_i = small2[:, 1, 0:NBLK].bitcast(I32)
        ntype_f = small3[:, 1, 0:NBLK]
        muv = small[:, 0, 0:NHEAD * NREL]
        kwb = T[0][:, 0:2 * NREL * D].rearrange("p (h c) -> p h c", h=2)

        def per_block(v):
            return v.unsqueeze(2).to_broadcast([P, NBLK, D])

        def per_feature(v):
            return v.unsqueeze(1).to_broadcast([P, NBLK, D])

        block = ctx.enter_context(nc.Block())

        @block.sync
        def _(sp):
            join = Join(sp)
            w = [0]

            def load(dst, src, **how):
                w[0] += 16
                sp.dma_start(dst, src, **how).then_inc(w_in, 16)

            def landed():
                sp.wait_ge(w_in, w[0])

            def rowbc(q, src):
                load(bc[:, q, :], src.rearrange("(a d) -> a d", a=1).to_broadcast([P, D]))

            def column(j, src):
                load(col[:, j:j + 1], src.rearrange("(d a) -> d a", a=1))

            def table(tab, src, n):
                sp.dma_start(tab.rearrange("(b p) d -> p b d", p=P), src).then_inc(t_out, 16)
                sp.wait_ge(t_out, 16 * n)

            sp.dma_start(dsti, a["dst"].rearrange("(p c) -> p c", p=EP)).then_inc(el_in, 16)
            sp.dma_start(srci, a["src"].rearrange("(p c) -> p c", p=EP)).then_inc(el_in, 16)
            sp.dma_start(eti, a["edge_type_5"].rearrange("(p c) -> p c", p=EP)).then_inc(el_in, 16)
            sp.wait_ge(x_pad, 1)
            load(X[:, 0:NBLK - 1, :], a["x"][0:(NBLK - 1) * P, :].rearrange("(b p) d -> p b d", p=P))
            load(X[0:LASTROWS, NBLK - 1, :], a["x"][(NBLK - 1) * P:N, :])
            rowbc(2, a["L0_gnn_be"][0])
            landed()
            sp.wait_ge(cst2, 3)
            rv = rec.rearrange("(g p s) r -> g p s r", p=P, s=FILL)
            for g in range(NT // FILL):
                sp.dma_start(rv[g], fillb).then_inc(fill_out, 16)
            sp.wait_ge(fill_out, 16 * (NT // FILL))
            sp.wait_ge(el_in, 48)
            join.to("slots")
            e64 = a["edge_attr_64"].rearrange("(p c) d -> p c d", p=EP)
            e32 = a["edge_attr_32"].rearrange("(p c) d -> p c d", p=EP)

            def rows_in(i, h, k):
                if late(k, 2):
                    sp.wait_ge(scat[h], i * (16 * SC))
                sp.dma_start(recb[:, h, :, 0:EA], e64[:, bass.ds(k * SC, SC), :]).then_inc(att_in[h], 16)
                sp.dma_start(recb[:, h, :, EA:EA + EB], e32[:, bass.ds(k * SC, SC), :]).then_inc(att_in[h], 16)
            halves(sp, rows_in, EC // SC)
            for h in range(2):
                sp.wait_ge(scat[h], 16 * SC * (EC // SC // 2))
            join.to("records")
            rt = rec.rearrange("(t p) r -> p t r", p=P)
            for l in range(3):
                load(wt[0:EA, 0:D], a["L0_gnn_We"][l])
                load(wt[:, D:2 * D], a["L0_gnn_W1"][l])
                load(wt[:, 2 * D:3 * D], a["L0_gnn_W2"][l])
                column(0, a["L0_gnn_b1"][l])
                column(1, a["L0_gnn_b2"][l])
                rowbc(0, a["L0_gnn_gamma"][l])
                rowbc(1, a["L0_gnn_beta"][l])
                if l < 2:
                    rowbc(2, a["L0_gnn_be"][l + 1])
                landed()
                table(tab0, T3[0], l + 1)
                join.to(f"weights{l}")

                def slots_in(t):
                    if t.late(4):
                        sp.wait_ge(qs["moved"], t.n - 3)
                    sp.dma_start(recin[:, t.s4], rt[:, bass.ds(t.k * B, B), :]).then_inc(rin[t.s4], 16)

                def attrs(t):
                    if t.late(2):
                        sp.wait_ge(qg["edge"], t.n - 1)
                    if l == 0:
                        sp.wait_ge(rout[t.h], t.i * 16 + 16)
                    sp.dma_start(ear[0:EA, t.h, :], eat[bass.ds(t.k, 1), 0:EA, :].rearrange("a p c -> p (a c)")).then_inc(qg.ea[t.h], 16)
                run(sp, [(0, slots_in), (4, attrs)] if l == 0 else [(0, attrs)], l)
                join.to(f"norm{l}")
            for r in range(NREL):
                load(wt[:, r * D:(r + 1) * D], a["L1_gnn_WV"][r])
                load(T[1][:, r * D:(r + 1) * D], a["WKT"][r])
                load(T[1][:, (NREL + r) * D:(NREL + r + 1) * D], a["WQT"][r])
            column(0, a["L1_gnn_a_vec"][D:2 * D])
            column(1, a["L1_gnn_a_vec"][0:D])
            landed()
            join.to("rel_vectors")
            t1v = tab1.rearrange("(b p r) w -> b p (r w)", p=P, r=NREL)
            for b in range(NBLK):
                sp.wait_ge(rows_rdy, 2 * (b + 1))
                sp.dma_start(t1v[b], T[2 + b % 2][:, 0:NREL * T1W]).then_inc(rows_out[b % 2], 16)
            sp.wait_ge(rows_out[0], 16 * 13)
            sp.wait_ge(rows_out[1], 16 * 12)
            join.to("tr_clear")
            for h in range(NHEAD):
                s = slice(h * HD, (h + 1) * HD)
                load(WQV[s, :, h * HD:(h + 1) * HD], a["L2_gnn_W_Q"][:, h].rearrange("t d f -> d t f"))
                load(WQV[s, :, D + h * HD:D + (h + 1) * HD], a["L2_gnn_W_V"][:, h].rearrange("t d f -> d t f"))
                load(WKb[s, :, s], a["L2_gnn_W_K"][:, h].rearrange("t d f -> d t f"))
                load(WEb[s, :, s], a["L2_gnn_W_edge"][:, h].rearrange("t d f -> d t f"))
            load(muv, a["L2_gnn_mu"].rearrange("h r -> (h r)").rearrange("(a c) -> a c", a=1).to_broadcast([P, NHEAD * NREL]))
            load(ntype_i[:, 0:NBLK - 1], a["node_type_3"][0:(NBLK - 1) * P].rearrange("(b p) -> p b", p=P),
                 allow_slow_non_contiguous=True)
            load(ntype_i[0:LASTROWS, NBLK - 1:NBLK], a["node_type_3"][(NBLK - 1) * P:N].rearrange("(p a) -> p a", a=1))
            landed()
            join.to("tr_qv")
            t2v = tab2k.rearrange("(b p r) w -> b p (r w)", p=P, r=NREL)
            for b in range(NBLK):
                sp.wait_ge(vals_rdy, 2 * (b + 1))
                sp.dma_start(t2v[b], kwb[:, b % 2, :]).then_inc(keys_out[b % 2], 16)
            sp.wait_ge(keys_out[0], 16 * 13)
            sp.wait_ge(keys_out[1], 16 * 12)
            table(tab2v, T3[4], 4)
            join.to("trB")
            load(wt[:, 0:D], a["L2_gnn_W_out"])
            load(wt[:, D:D + FF], a["L2_gnn_W1"])
            load(wt[:, D + FF:D + 2 * FF].rearrange("p (c n) -> p c n", c=4), a["L2_gnn_W2"].rearrange("(c p) n -> p c n", p=P))
            column(0, a["L2_gnn_b_out"])
            for c in range(4):
                column(1 + c, a["L2_gnn_b1"][c * P:(c + 1) * P])
            column(5, a["L2_gnn_b2"])
            rowbc(0, a["L2_gnn_ln1_g"])
            rowbc(1, a["L2_gnn_ln1_b"])
            landed()
            join.to("tr_norm1")
            rowbc(0, a["L2_gnn_ln2_g"])
            rowbc(1, a["L2_gnn_ln2_b"])
            landed()
            join.to("tr_out")
            load(wt[0:EB, 0:D], a["W3T"][2 * D:2 * D + EB, :])
            load(wt[:, D:2 * D], a["W3T"][0:D, :])
            load(wt[:, 2 * D:3 * D], a["W3T"][D:2 * D, :])
            load(wt[:, 3 * D:4 * D], a["W32T"])
            load(wt[:, 4 * D:5 * D], a["WuT"])
            column(0, a["L3_gnn_bu"])
            load(b2row[:, :], a["L3_gnn_b2"].rearrange("(a d) -> a d", a=1))
            rowbc(0, a["L3_gnn_gamma"])
            rowbc(1, a["L3_gnn_beta"])
            rowbc(2, a["L3_gnn_b1"])
            landed()
            join.to("mp_node")
            table(tab3, T3[1], 5)
            join.to("mp_table")

            def attrs3(t):
                if t.late(2):
                    sp.wait_ge(qp["node"], t.n - 1)
                sp.dma_start(ear[0:EB, t.h, :], eat[bass.ds(t.k, 1), EA:EAB, :].rearrange("a p c -> p (a c)")).then_inc(qp.ea[t.h], 16)
            run(sp, [(0, attrs3)])
            join.to("mp_out")
            ov = out[0:(NBLK - 1) * P, :].rearrange("(b p) d -> p b d", p=P)
            sp.dma_start(ov, X[:, 0:NBLK - 1, :]).then_inc(fin, 16)
            sp.dma_start(out[(NBLK - 1) * P:N, :], X[0:LASTROWS, NBLK - 1, :]).then_inc(fin, 16)
            sp.wait_ge(fin, 32)

        @block.gpsimd
        def _(pool):
            join = Join(pool)
            pool.memset(ones[:, :], 1.0).then_inc(cst, 1)
            pool.iota(idx5[:, 0:NT], pattern=[[1, NT]], base=0, channel_multiplier=0).then_inc(cst, 1)
            pool.memset(ident[:, :], 0.0).then_inc(cst, 1)
            pool.memset(tri[:, :], 1.0).then_inc(cst, 1)
            pool.memset(fillb, 0.0).then_inc(cst2, 1)
            pool.wait_ge(cst2, 1)
            pool.memset(fillb[:, :, EA + EB + 1:EA + EB + 2], -1.0).then_inc(cst2, 1)
            pool.iota(iota_pi, pattern=[[0, 1]], base=0, channel_multiplier=1).then_inc(cst2, 1)
            pool.wait_ge(cst, 4)
            pool.affine_select(out=ident[:, :], in_=ident[:, :], compare_op=ALU.not_equal, fill=1.0, base=0,
                               pattern=[[-1, P]], channel_multiplier=1).then_inc(cst, 1)
            pool.affine_select(out=tri[:, :], in_=tri[:, :], compare_op=ALU.is_gt, fill=0.0, base=0,
                               pattern=[[1, P]], channel_multiplier=-1).then_inc(cst, 1)
            join.to("slots")

            def scatter(i, h, k):
                pool.wait_ge(rec_rdy, k + 1)
                pool.sem_inc(pool_go, 1)
                for c in range(SC):
                    pool.indirect_dma_start(
                        out=rec[:, :], out_offset=bass.IndirectOffsetOnAxis(ap=slotr[0:EP, h, c:c + 1], axis=0),
                        in_=recb[:, h, c, :], in_offset=None).then_inc(scat[h], 16)
            halves(pool, scatter, EC // SC)

            def gathers(q, free, table, width, of=0):
                def body(t):
                    pool.wait_ge(q["index"], t.n + 1)
                    if t.late(4):
                        pool.wait_ge(q[free], t.n - 3)
                    pool.sem_inc(pool_go, 1)
                    for j in range(B):
                        pool.indirect_dma_start(
                            out=ring[:, t.s4, j, 0:width], out_offset=None, in_=table[:, :],
                            in_offset=bass.IndirectOffsetOnAxis(ap=idxr[:, t.s4, j:j + 1], axis=0)).then_inc(q.gath[t.s4], 16)
                run(pool, [(0, body)], of)

            for l in range(3):
                join.to(f"weights{l}")
                gathers(qg, "added", tab0, D, l)
            join.to("rel_table")
            gathers(qm, "scores", tab1, T1W)
            join.to("rel_den")
            gathers(qr, "messages", tab1, T1W)
            join.to("tr_values")
            gathers(qm, "scores", tab2k, D, 1)
            join.to("tr_zero")
            gathers(qt, "messages", tab2v, D)
            join.to("mp_table")
            gathers(qp, "added", tab3, D)
            join.to("mp_out")

        @block.vector
        def _(dve):
            join = Join(dve)
            ch = Chain(dve, dve_ch)
            V = nc.vector
            norms = [0]

            def tt(o, x, y, op):
                return V.tensor_tensor(o, x, y, op)

            def norm(src, dst, sq, relu=False, gb=False):
                ch(V.reduce_sum(stat[:, 0, 0:NBLK], src, AX))
                ch(V.tensor_scalar(stat[:, 0, 0:NBLK], stat[:, 0, 0:NBLK], 1.0 / D, None, ALU.mult))
                ch(tt(dst, src, per_block(stat[:, 0, 0:NBLK]), ALU.subtract))
                ch(tt(sq, dst, dst, ALU.mult))
                ch(V.reduce_sum(stat[:, 1, 0:NBLK], sq, AX))
                ch(V.tensor_scalar(stat[:, 1, 0:NBLK], stat[:, 1, 0:NBLK], 1.0 / D, LN_EPS, ALU.mult, ALU.add))
                norms[0] += 1
                dve.sem_inc(ln_var, 1)
                dve.wait_ge(ln_std, norms[0])
                ch(V.reciprocal(stat[:, 3, 0:NBLK], stat[:, 2, 0:NBLK]))
                ch(tt(dst, dst, per_block(stat[:, 3, 0:NBLK]), ALU.mult))
                if relu:
                    ch(V.tensor_scalar(dst, dst, 0.0, None, ALU.max))
                if gb:
                    ch(tt(dst, dst, per_feature(bc[:, 0, :]), ALU.mult))
                    ch(tt(dst, dst, per_feature(bc[:, 1, :]), ALU.add))

            dve.wait_ge(cst, 6)
            dve.wait_ge(cst2, 3)
            ch(V.tensor_copy(iota_p, iota_pi))
            ch(V.tensor_copy(iota_t, idx5[:, 0:NT]))
            ch(V.tensor_copy(iota_n[:, :], idx5[:, 0:P]))
            ch(V.memset(X[:, NBLK - 1, :], 0.0))
            dve.sem_inc(x_pad, 1)
            ch(V.memset(ne[:, :, :], 1.0))
            ch(V.memset(zero, 0.0))
            ch(V.memset(slotf, 0.0))
            ch(V.memset(nbf, 0.0))
            ch(V.memset(idx1[:, :], 0))
            ch(V.memset(idx5[:, :], 0))
            dve.wait_ge(el_in, 48)
            ch(V.tensor_single_scalar(bki, dsti, 7, ALU.arith_shift_right))
            ch(V.tensor_copy(bkf, bki))
            ch(V.tensor_copy(dstf, dsti))
            ch(V.tensor_copy(fields[:, :, 0], srci))
            ch(V.scalar_tensor_tensor(fields[:, :, 1], bkf, -float(P), dstf, ALU.mult, ALU.add))
            ch(V.tensor_copy(fields[:, :, 2], eti))
            ch(V.scalar_tensor_tensor(fields[:, :, 3], fields[:, :, 0], float(NREL), fields[:, :, 2], ALU.mult, ALU.add))

            def count(b):
                ch(V.tensor_scalar(mask, bkf, iota_n[0:EP, bass.ds(b, 1)], None, ALU.is_equal))
                ch(V.tensor_tensor_scan(tmp, mask, zero, 0.0, ALU.add, ALU.add))
                ch(V.tensor_scalar(cum[:, bass.ds(b, 1), :].rearrange("p a c -> p (a c)"), tmp, 0.0, None, ALU.add))
                ch(V.tensor_scalar(cnt[0:EP, bass.ds(b, 1)], tmp[:, EC - 1:EC], 0.0, None, ALU.add))
            ch.loop(0, NBLK, count)
            dve.sem_inc(cnt_rdy, 1)
            dve.wait_ge(cnt_ps, 1)
            ch(V.tensor_copy(prefix[0:EP], ps[0:EP, 0, 0:NBLK]))
            ch(V.tensor_scalar(tot, ps[:, 1, 0:NBLK], float(P - 1), None, ALU.add))
            ch(V.tensor_copy(nt_i, tot))
            ch(V.tensor_single_scalar(nt_i, nt_i, 7, ALU.arith_shift_right))
            ch(V.tensor_copy(nt_f, nt_i))
            ch(V.memset(off, 0.0))
            ch(V.tensor_tensor_scan(wend, nt_f, off, 0.0, ALU.add, ALU.add))
            ch(tt(wst, wend, nt_f, ALU.subtract))
            ch(V.tensor_scalar(off[0:EP], wst[0:EP], float(P), -1.0, ALU.mult, ALU.add))
            ch(tt(off[0:EP], off[0:EP], prefix[0:EP], ALU.add))

            def place(b):
                ch(V.tensor_scalar(mask, bkf, iota_n[0:EP, bass.ds(b, 1)], None, ALU.is_equal))
                ch(V.scalar_tensor_tensor(tmp, cum[:, bass.ds(b, 1), :].rearrange("p a c -> p (a c)"),
                                          off[0:EP, bass.ds(b, 1)], mask, ALU.add, ALU.mult))
                ch(tt(slotf, slotf, tmp, ALU.add))
                ch(V.scalar_tensor_tensor(nbf, iota_t, wend[:, bass.ds(b, 1)], nbf, ALU.is_ge, ALU.add))
            ch.loop(0, NBLK, place)
            ch(V.tensor_copy(slot, slotf))
            ch(V.tensor_scalar(nbf, nbf, float(NBLK - 1), None, ALU.min))
            ch(V.tensor_copy(nb[:, :], nbf))
            join.to("slots")

            def build_rows(i, h, k):
                dve.wait_ge(att_in[h], i * 32 + 32)
                if late(k, 2):
                    dve.wait_ge(scat[h], i * (16 * SC))
                V.tensor_scalar(slotr[0:EP, h, :], slot[:, bass.ds(k * SC, SC)], 0.0, None, ALU.add).then_inc(rows_ch, 1)
                V.tensor_scalar(recb[:, h, :, EA + EB:REC], fields[:, bass.ds(k * SC, SC), :], 0.0, None,
                                ALU.add).then_inc(rows_ch, 1)
                dve.wait_ge(rows_ch, k * 2 + 2)
                dve.sem_inc(rec_rdy, 1)
            halves(dve, build_rows, EC // SC)
            norm(X[:, :, :], H[:, :, :], T3[1], relu=True)
            ch(tt(T3[0], H[:, :, :], per_feature(bc[:, 2, :]), ALU.add))
            join.to("records")
            ch(V.tensor_copy(XL, H[:, :, :]))


            def onehot(q, t, free=None):
                if free and t.late(4):
                    dve.wait_ge(q[free], t.n - 3)
                tt(oh[:, t.s4], iota_n[:, :].unsqueeze(1).to_broadcast([P, B, P]),
                   dl[:, bass.ds(t.k * B, B)].unsqueeze(2).to_broadcast([P, B, P]), ALU.is_equal).then_inc(q["onehot"], 1)

            def accumulate(q, t, dst, src, op=ALU.add):
                blocks = blocks_of(dve, DVE, t)
                for j in range(B):
                    if t.late(1) or j:
                        dve.wait_ge(q["acc"], t.n * B + j)
                    o = dst(blocks[j])
                    tt(o, o, src(j), op).then_inc(q["acc"], 1)

            def into(agg, w):
                return lambda b: agg[:, bass.ds(b, 1), 0:w].rearrange("p a w -> p (a w)")

            def flat(v):
                return v.rearrange("p j d -> p (j d)")

            sort = Steps(dve, qs["chain"], 4)

            def sort_keys(t):
                sort.start(t.n)
                dve.wait_ge(rin[t.s4], t.u * 16 + 16)
                f = recin[:, t.s4]
                key = small2[:, t.s4, 0:B]
                if t.late(4):
                    dve.wait_ge(qs["spread"], t.n - 3)
                sort(V.scalar_tensor_tensor(key, f[:, :, EAB + 1], 8.0, f[:, :, EAB + 2], ALU.mult, ALU.add))
                sort(V.tensor_scalar(key, key, float(P), iota_p, ALU.mult, ALU.add))
                dve.sem_inc(qs["keys"], 1)

            def sort_places(t):
                dve.wait_ge(qs["spread"], t.n + 1)
                tt(keyT[:, t.h], ps[:, 6 + t.h, :].rearrange("p (j d) -> p j d", j=B),
                   small2[:, t.s4, 0:B].unsqueeze(2).to_broadcast([P, B, P]), ALU.is_lt).then_inc(rank_sem, 1)
                dve.wait_ge(rank_sem, t.n * 2 + 1)
                V.reduce_sum(small3[:, t.s4, 0:B], keyT[:, t.h], AX).then_inc(rank_sem, 1)
                dve.wait_ge(rank_sem, t.n * 2 + 2)
                if t.late(2):
                    dve.wait_ge(qs["moved"], t.n - 1)
                tt(perm[:, t.h], iota_n[:, :].unsqueeze(1).to_broadcast([P, B, P]),
                   small3[:, t.s4, 0:B].unsqueeze(2).to_broadcast([P, B, P]), ALU.is_equal).then_inc(qs["perm"], 1)

            def sort_fields(t):
                sort2.start(t.n)
                dve.wait_ge(qs["moved"], t.n + 1)
                f = ps[:, 5, t.h * 64:t.h * 64 + 4 * B].rearrange("p (j c) -> p j c", j=B)
                for dst, c in ((idx1, 0), (dl, 1), (et, 2), (idx5, 3)):
                    ins = V.tensor_scalar(dst[:, bass.ds(t.k * B, B)], f[:, :, c], 0.0, None, ALU.add)
                    sort2(ins)
                dve.sem_inc(qs["fields"], 1)

            def acc_gine(t):
                dve.wait_ge(qg["sums"], t.n + 1)
                accumulate(qg, t, into(XL, D), lambda j: ps[:, 2 + t.h, j * P:(j + 1) * P])

            def add_gine(t):
                dve.wait_ge(qg.gath[t.s4], t.u * (16 * B) + 16 * B)
                dve.wait_ge(qg["edge"], t.n + 1)
                if t.late(2):
                    dve.wait_ge(qg["relu"], t.n - 1)
                tt(mraw[:, t.h], ps[:, t.h, :].rearrange("p (j d) -> p j d", j=B), ring[:, t.s4, :, 0:D], ALU.add).then_inc(qg["added"], 1)

            for l in range(3):
                join.to(f"weights{l}")
                one = lambda t: onehot(qg, t, "sums")
                if l == 0:
                    sort = Steps(dve, qs["chain"], 2)
                    sort2 = Steps(dve, sort2_sem, 4)
                    run(dve, [(8, acc_gine), (6, add_gine), (0, sort_keys), (1, sort_places), (2, sort_fields), (4, one)], l)
                else:
                    run(dve, [(3, acc_gine), (0, one), (1, add_gine)], l)
                dve.wait_ge(qg["acc"], NB * B * (l + 1))
                join.to(f"out{l}")
                norm(T3[4], T3[3], T3[1], gb=True)
                if l < 2:
                    ch(V.tensor_copy(XL, T3[3]))
                    ch(tt(T3[0], T3[3], per_feature(bc[:, 2, :]), ALU.add))
                else:
                    ch(tt(X[:, :, :], X[:, :, :], T3[3], ALU.add))
                    norm(X[:, :, :], H[:, :, :], T3[1], relu=True)
                    ch(V.memset(aren[:, 2 * NPAD:4 * NPAD], 0.0))
                join.to(f"norm{l}")

            join.to("rel_T")
            dve.wait_ge(relv_ps, 1)
            ch(V.tensor_copy(wt[:, NREL * D:NREL * D + 2 * NREL], ps[:, 4, 0:2 * NREL]))
            ch(V.memset(MX[:, :, :], -BIG))
            join.to("rel_table")

            def types(o, t):
                return tt(o, iota_n[:, 0:NREL].unsqueeze(1).to_broadcast([P, B, NREL]),
                          et[:, bass.ds(t.k * B, B)].unsqueeze(2).to_broadcast([P, B, NREL]), ALU.is_equal)

            def batch_of(v, w):
                return v.rearrange("p (j r) -> p j r", j=B) if w else v

            ch_scan, ch_acc = Steps(dve, qm["ch_scan"], 4), Steps(dve, qm["ch_acc"], 2)

            def scan_max(n):
                def body(t):
                    ch_scan.start(t.n)
                    rows = B * n
                    z, key = tz[0:rows, t.h, 0:P], tz[0:rows, t.h, P:2 * P]
                    reset, f, start = sf[0:rows, t.h, 0:P], sf[0:rows, t.h, P:2 * P], ne[0:rows, t.h, :]
                    dve.wait_ge(qm["rows_sb"], t.n + 1)
                    if t.late(2):
                        dve.wait_ge(qm["back"], t.n - 1)
                    ch_scan(tt(start[:, 1:P], key[:, 1:P], key[:, 0:P - 1], ALU.not_equal))
                    ch_scan(V.tensor_scalar(reset, start[:, 0:P], -4 * BIG, None, ALU.mult))
                    ch_scan(V.tensor_tensor_scan(f, reset, z, 0.0, ALU.add, ALU.max))
                    ch_scan(tt(f, f, start[:, 1:P + 1], ALU.mult))
                    dve.sem_inc(qm["scanned"], 1)
                return body

            def acc_max(n, per_type):
                def body(t):
                    ch_acc.start(t.n)
                    dve.wait_ge(qm["sums"], t.n + 1)
                    w = 2 * NREL if per_type else n + 1
                    got = ps[:, 7, t.h * 64:t.h * 64 + B * w].rearrange("p (j c) -> p j c", j=B)
                    m = NREL if per_type else 1
                    miss = small4[:, t.s4, 0:B * m].rearrange("p (j c) -> p j c", j=B)
                    cand = small4[:, t.s4, 24:24 + B * n].rearrange("p (j c) -> p j c", j=B)
                    ch_acc(V.tensor_scalar(miss, got[:, :, n:n + m], BIG, -BIG, ALU.mult, ALU.add))
                    ch_acc(tt(cand, got[:, :, 0:n], miss if per_type else miss.to_broadcast([P, B, n]), ALU.add))
                    accumulate(qm, t, into(MX, n), lambda j: cand[:, j, :], ALU.max)
                return body

            ch_rel = Steps(dve, qm["ch_score"], 4)

            def rel_score(t):
                ch_rel.start(t.n)
                dve.wait_ge(qm.gath[t.s4], t.u * (16 * B) + 16 * B)
                if t.late(4):
                    dve.wait_ge(qm["rows"], t.n - 3)
                sk = ring[:, t.s4, :, D]
                ch_rel(V.tensor_scalar(small3[:, t.s4, 0:B], sk, 0.0, None, ALU.add))
                ch_rel(V.tensor_scalar(SK[:, bass.ds(t.k * B, B)], sk, 0.0, None, ALU.add))
                ch_rel(V.scalar_tensor_tensor(small3[:, t.s4, 32:32 + B], dl[:, bass.ds(t.k * B, B)], 8.0,
                                              et[:, bass.ds(t.k * B, B)], ALU.mult, ALU.add))
                ch_rel(types(small2[:, t.s4, 0:B * NREL].rearrange("p (j r) -> p j r", j=B), t))
                dve.sem_inc(qm["scores"], 1)

            def rel_pick(t):
                dve.wait_ge(qm["back"], t.n + 1)
                R = small2[:, t.s4, 0:B * NREL].rearrange("p (j r) -> p j r", j=B)
                if t.late(4):
                    dve.wait_ge(qm["sums"], t.n - 3)
                for c in range(2):
                    src = ps[:, 6, t.h * 128 + c * 32:t.h * 128 + c * 32 + B].unsqueeze(2).to_broadcast([P, B, NREL])
                    ins = tt(gm[:, t.s4, :, c * NREL:(c + 1) * NREL], R, src, ALU.mult)
                ins.then_inc(qm["picked"], 1)

            run(dve, [(5, acc_max(NREL, True)), (3, rel_pick), (1, rel_score), (0, lambda t: onehot(qm, t, "sums")), (2, scan_max(1))])
            dve.wait_ge(qm["acc"], NB * B)
            mxv, c1m = MX[:, :, 0:NREL], C1[:, :, NREL:2 * NREL]
            ch(tt(mxv, mxv, C1[:, :, 0:NREL], ALU.add))
            ch(V.scalar_tensor_tensor(c1m, mxv, 0.2, mxv, ALU.mult, ALU.max))
            ch(V.memset(DEN, 0.0))
            join.to("rel_max")

            ch_d = Steps(dve, qd["chain"], 9)

            def rel_logit(t):
                ch_d.start(t.n)
                w = B * NREL
                R = small[:, t.s4, 0:w].rearrange("p (j r) -> p j r", j=B)
                ch_d(types(R, t))
                dve.wait_ge(qd["node"], t.n + 1)
                s, m, p = (small3[:, t.s4, c * B:(c + 1) * B] for c in range(3))
                for c, o in ((0, s), (1, m)):
                    pick = small2[:, t.s4, c * w:(c + 1) * w].rearrange("p (j r) -> p j r", j=B)
                    nd = ps[:, 2 + t.h, 0:B * 2 * NREL].rearrange("p (j c r) -> p j c r", j=B, c=2)[:, :, c, :]
                    ch_d(tt(pick, nd, R, ALU.mult))
                    ch_d(V.reduce_sum(o, pick, AX))
                ch_d(tt(s, s, SK[:, bass.ds(t.k * B, B)], ALU.add))
                ch_d(V.scalar_tensor_tensor(s, s, 0.2, s, ALU.mult, ALU.max))
                ch_d(tt(s, s, m, ALU.subtract))
                ch_d(V.tensor_scalar(s, s, 0.0, None, ALU.min))
                dve.sem_inc(qd["logits"], 1)

            ch_w = Steps(dve, qd["chain2"], 2)

            def rel_weight(t):
                ch_w.start(t.n)
                R = small[:, t.s4, 0:B * NREL].rearrange("p (j r) -> p j r", j=B)
                p = small3[:, t.s4, 2 * B:3 * B]
                dve.wait_ge(qd["exp"], t.n + 1)
                ch_w(V.tensor_scalar(PW[:, bass.ds(t.k * B, B)], p, 0.0, None, ALU.add))
                if t.late(4):
                    dve.wait_ge(qd["sums"], t.n - 3)
                ch_w(tt(gm[:, t.s4, :, 0:NREL], R, p.unsqueeze(2).to_broadcast([P, B, NREL]), ALU.mult))
                dve.sem_inc(qd["weights"], 1)

            def acc_den(t):
                dve.wait_ge(qd["sums"], t.n + 1)
                accumulate(qd, t, into(DEN, NREL), lambda j: ps[:, 4 + t.h, j * NREL:(j + 1) * NREL])

            run(dve, [(5, acc_den), (3, rel_weight), (2, rel_logit), (0, lambda t: onehot(qd, t, "sums"))])
            dve.wait_ge(qd["acc"], NB * B)
            ch(V.tensor_scalar(DEN, DEN, 1e-10, None, ALU.add))
            ch(V.reciprocal(C1[:, :, 0:NREL], DEN))
            ch(V.memset(AG[:, :], 0.0))
            join.to("rel_den")

            ch_r = Steps(dve, qr["chain"], 4)

            def rel_message(t):
                ch_r.start(t.n)
                R = small[:, t.s4, 0:B * NREL].rearrange("p (j r) -> p j r", j=B)
                pick = small2[:, t.s4, 0:B * NREL].rearrange("p (j r) -> p j r", j=B)
                w = small3[:, t.s4, 0:B]
                ch_r(types(R, t))
                dve.wait_ge(qr["node"], t.n + 1)
                ch_r(tt(pick, ps[:, 2 + t.h, 0:B * NREL].rearrange("p (j r) -> p j r", j=B), R, ALU.mult))
                ch_r(V.reduce_sum(w, pick, AX))
                ch_r(tt(w, w, PW[:, bass.ds(t.k * B, B)], ALU.mult))
                dve.wait_ge(qr.gath[t.s4], t.u * (16 * B) + 16 * B)
                if t.late(4):
                    dve.wait_ge(qr["sums"], t.n - 3)
                tt(msg[:, t.s4, :, 0:D], ring[:, t.s4, :, 0:D], w.unsqueeze(2).to_broadcast([P, B, D]), ALU.mult).then_inc(qr["messages"], 1)

            def acc_pair(q, agg, w):
                def body(t):
                    dve.wait_ge(q["sums"], t.n + 1)
                    accumulate(q, t, into(agg, w), lambda j: ps[:, 4 + 2 * t.h + j // 2, (j % 2) * 256:(j % 2) * 256 + w])
                return body

            run(dve, [(4, acc_pair(qr, agg2, D)), (2, rel_message), (0, lambda t: onehot(qr, t, "sums"))])
            dve.wait_ge(qr["acc"], NB * B)
            hp, neg = agg2[:, :, 0:D], T3[0]
            ch(V.tensor_scalar(neg, hp, 0.0, None, ALU.min))
            dve.sem_inc(elu_in, 1)
            ch(V.tensor_scalar(hp, hp, 0.0, -1.0, ALU.max, ALU.add))
            ch(tt(X[:, :, :], X[:, :, :], hp, ALU.add))
            dve.wait_ge(elu_exp, 1)
            ch(tt(X[:, :, :], X[:, :, :], neg, ALU.add))
            norm(X[:, :, :], H[:, :, :], XL, relu=True)
            join.to("rel_out")

            ch(V.memset(wt[:, 0:WK_o + NTYPE * D], 0.0))
            ch(V.memset(WE, 0.0))
            ch(V.memset(ntype_i, 0))
            ch(V.memset(MX[:, :, :], -BIG))
            join.to("tr_weights")
            ch(V.tensor_scalar(muv, muv, float(HD) ** -0.5, None, ALU.mult))
            ch(V.tensor_copy(ntype_f, ntype_i))
            for t, o in ((0, T3[3]), (1, T3[4]), (2, XL)):
                ch(V.tensor_scalar(stat[:, t, 0:NBLK], ntype_f, float(t), None, ALU.is_equal))
                ch(tt(o, H[:, :, :], per_block(stat[:, t, 0:NBLK]), ALU.mult))
            join.to("tr_masked")
            join.to("tr_qv")
            for b in range(NBLK):
                for part, r0, nr in ((0, 0, 4), (1, 4, 1)):
                    dve.wait_ge(kw_ps, 2 * b + part + 1)
                    if b >= 2:
                        dve.wait_ge(keys_out[b % 2], 16 * (b // 2))
                    for r in range(r0, r0 + nr):
                        ins = tt(kwb[:, b % 2, r * D:(r + 1) * D].rearrange("p (h d) -> p h d", h=NHEAD),
                                 ps[:, 4 + 2 * (b % 2) + part, (r - r0) * D:(r - r0 + 1) * D].rearrange("p (h d) -> p h d", h=NHEAD),
                                 muv.rearrange("p (h r) -> p h r", h=NHEAD)[:, :, r:r + 1].to_broadcast([P, NHEAD, HD]), ALU.mult)
                    ins.then_inc(vals_rdy, 1)
            dve.wait_ge(vals_rdy, 2 * NBLK)
            join.to("tr_values")
            ch_tr = Steps(dve, trs_sem, 4)

            def tr_score(t):
                ch_tr.start(t.k)
                s = small3[:, t.s4, 0:B * NHEAD]
                if t.late(4):
                    dve.wait_ge(qm["rows"], t.n - 3)
                ch_tr(V.tensor_scalar(small3[:, t.s4, 32:64].rearrange("p (j g) -> p j g", j=B),
                                      dl[:, bass.ds(t.k * B, B)].unsqueeze(2).to_broadcast([P, B, NHEAD]), 0.0, None, ALU.add))
                dve.wait_ge(qm.gath[t.s4], t.u * (16 * B) + 16 * B)
                dve.wait_ge(qm["node"], t.k + 1)
                ch_tr(tt(mraw[:, t.h], ps[:, 2 + t.h, :].rearrange("p (j d) -> p j d", j=B), ring[:, t.s4, :, 0:D], ALU.mult))
                ch_tr(V.reduce_sum(s.rearrange("p (g a) -> p g a", a=1), mraw[:, t.h].rearrange("p j (g d) -> p (j g) d", d=HD), AX))
                dve.sem_inc(qm["scores"], 1)
                ch_tr(V.tensor_scalar(score[:, bass.ds(t.k * (B * NHEAD), B * NHEAD)], s, 0.0, None, ALU.add))

            run(dve, [(5, acc_max(NHEAD, False)), (2, tr_score), (0, lambda t: onehot(qm, t, "sums")), (3, scan_max(NHEAD))], 1)
            dve.wait_ge(qm["acc"], 2 * NB * B)
            join.to("trA")
            ch(V.memset(AG[:, :], 0.0))
            join.to("tr_zero")

            def tr_logit(t):
                dve.wait_ge(qt["node"], t.n + 1)
                if t.late(4):
                    dve.wait_ge(qt["exp"], t.n - 3)
                tt(small3[:, t.s4, 0:B * NHEAD], score[:, bass.ds(t.k * (B * NHEAD), B * NHEAD)],
                   ps[:, 2 + t.h, 0:B * NHEAD], ALU.subtract).then_inc(qt["logits"], 1)

            def tr_message(t):
                dve.wait_ge(qt["exp"], t.n + 1)
                dve.wait_ge(qt.gath[t.s4], t.u * (16 * B) + 16 * B)
                for j in range(B):
                    ins = tt(msg[:, t.s4, j, 0:D].rearrange("p (g d) -> p g d", g=NHEAD),
                             ring[:, t.s4, j, 0:D].rearrange("p (g d) -> p g d", g=NHEAD),
                             msg[:, t.s4, j, D:W2N].unsqueeze(2).to_broadcast([P, NHEAD, HD]), ALU.mult)
                ins.then_inc(qt["messages"], 1)

            run(dve, [(5, acc_pair(qt, agg2, W2N)), (3, tr_message), (2, tr_logit), (0, lambda t: onehot(qt, t, "sums"))])
            dve.wait_ge(qt["acc"], NB * B)
            join.to("trB")
            den = agg2[:, :, D:W2N]
            rden = T[4][:, 0:NBLK * NHEAD].rearrange("p (b g) -> p b g", b=NBLK)
            ch(V.tensor_scalar(rden, den, 1e-10, None, ALU.add))
            ch(V.reciprocal(rden, rden))
            for g in range(NHEAD):
                s = slice(g * HD, (g + 1) * HD)
                ch(tt(T3[0][:, :, s], agg2[:, :, s], rden[:, :, g:g + 1].to_broadcast([P, NBLK, HD]), ALU.mult))
            join.to("tr_mix")
            ch(tt(T3[2], T3[3], H[:, :, :], ALU.add))
            norm(T3[2], T3[0], T3[1], gb=True)
            join.to("tr_norm1")
            join.to("tr_ff")
            ch(tt(T3[3], T3[3], T3[0], ALU.add))
            norm(T3[3], T3[1], T3[2], gb=True)
            ch(tt(X[:, :, :], X[:, :, :], T3[1], ALU.add))
            norm(X[:, :, :], H[:, :, :], T3[1], relu=True)
            ch(V.memset(AG[:, :], 0.0))
            ch(V.memset(msg[:, :, :, D:D + 1], 1.0))
            ch(V.memset(wt[:, 0:D], 0.0))
            ch(V.memset(ear[:, :, :], 0.0))
            join.to("tr_out")

            join.to("mp_T")
            for g in range((NBLK + 3) // 4):
                n = min(4, NBLK - 4 * g)
                dve.wait_ge(nt_ps, g + 1)
                tt(T3[2][:, 4 * g:4 * g + n, :], ps[:, 4 + g % 2, 0:n * P].rearrange("p (b d) -> p b d", b=n),
                   bc[:, 2, :].unsqueeze(1).to_broadcast([P, n, D]), ALU.add).then_inc(nt_free, 1)
            dve.wait_ge(nt_free, (NBLK + 3) // 4)
            join.to("mp_table")

            def mp_add(t):
                dve.wait_ge(qp.gath[t.s4], t.u * (16 * B) + 16 * B)
                dve.wait_ge(qp["node"], t.n + 1)
                if t.late(2):
                    dve.wait_ge(qp["relu"], t.n - 1)
                tt(mraw[:, t.h], ps[:, 2 + t.h, :].rearrange("p (j d) -> p j d", j=B), ring[:, t.s4, :, 0:D], ALU.add).then_inc(qp["added"], 1)

            run(dve, [(4, acc_pair(qp, agg3, D + 1)), (2, mp_add), (0, lambda t: onehot(qp, t, "sums"))])
            dve.wait_ge(qp["acc"], NB * B)
            join.to("mp_upd")
            ch(tt(T3[3], T3[2], H[:, :, :], ALU.add))
            norm(T3[3], T3[0], T3[4], gb=True)
            ch(tt(X[:, :, :], X[:, :, :], T3[0], ALU.add))
            join.to("mp_out")

        @block.scalar
        def _(act):
            join = Join(act)
            A = nc.scalar
            pn = [0]
            norms = [0]

            def evac(dst, func, bias=0.0, n=1, width=None):
                act.wait_ge(pn_full, pn[0] + 1)
                src = ps[:, 2 * (pn[0] % 2), 0:width]
                A.activation(dst, src, func, bias=bias).then_inc(pn_free, 1)
                pn[0] += 1

            def turned(dst):
                for g in range((NBLK + 3) // 4):
                    n = min(4, NBLK - 4 * g) * P
                    evac(dst[:, g * 512:g * 512 + n], ACT.Copy, width=n)
                act.wait_ge(pn_free, pn[0])

            def product(dst, func, bias):
                for g in range(NG):
                    evac(dst[:, g * G:(g + 1) * G], func, bias, width=G)
                act.wait_ge(pn_free, pn[0])

            def root():
                norms[0] += 1
                act.wait_ge(ln_var, norms[0])
                A.activation(stat[:, 2, 0:NBLK], stat[:, 1, 0:NBLK], ACT.Sqrt).then_inc(ln_std, 1)

            join.to("slots")
            root()

            def stage_indices(q, idx, first=0):
                def body(t):
                    if t.late(4):
                        act.wait_ge(q.gath[t.s4], t.u * (16 * B))
                    if first:
                        act.wait_ge(qs["fields"], t.n + 1)
                    act.sem_inc(act_go, 1)
                    A.copy(idxr[:, t.s4, :], idx[:, bass.ds(t.k * B, B)]).then_inc(q["index"], 1)
                return body

            def relu(q):
                def body(t):
                    act.wait_ge(q["added"], t.n + 1)
                    if t.late(4):
                        act.wait_ge(q["sums"], t.n - 3)
                    A.activation(msg[:, t.s4, :, 0:D], mraw[:, t.h], ACT.Relu).then_inc(q["relu"], 1)
                return body

            def attrs_out(t):
                act.wait_ge(qs["moved"], t.n + 1)
                if t.late(2):
                    act.wait_ge(rout[t.h], t.i * 16)
                A.activation(eato[:, t.h, :], ps[0:EAB, 4, :], ACT.Copy).then_inc(qs["attr_sb"], 1)
                act.wait_ge(qs["attr_sb"], t.n + 1)
                act.dma_start(eat[bass.ds(t.k, 1), :, :].rearrange("a p c -> p (a c)"), eato[:, t.h, :]).then_inc(rout[t.h], 16)

            for l in range(3):
                join.to(f"weights{l}")
                if l == 0:
                    run(act, [(2, attrs_out), (3, stage_indices(qg, idx1, 1)), (6, relu(qg))], l)
                    for h in range(2):
                        act.wait_ge(rout[h], 16 * (NB // 2))
                else:
                    run(act, [(0, stage_indices(qg, idx1)), (2, relu(qg))], l)
                join.to(f"gine{l}")
                turned(T[1])
                join.to(f"sumT{l}")
                product(T[2], ACT.Relu, col[:, 0:1])
                join.to(f"hiddenT{l}")
                product(T[3], ACT.Relu, col[:, 1:2])
                join.to(f"outT{l}")
                turned(T[4])
                join.to(f"out{l}")
                root()
                if l == 2:
                    root()
            join.to("rel_weights")
            turned(T[0])
            join.to("rel_vectors")
            for b in range(NBLK):
                rows = T[2 + b % 2][:, 0:NREL * T1W].rearrange("p (r w) -> p r w", r=NREL)
                if b >= 2:
                    act.wait_ge(rows_out[b % 2], 16 * (b // 2))
                act.wait_ge(pn_full, pn[0] + 1)
                s = 2 * (pn[0] % 2)
                A.activation(rows[:, 0:4, 0:D], ps[:, s, :].rearrange("p (r d) -> p r d", r=4), ACT.Copy).then_inc(rows_rdy, 1)
                A.activation(rows[:, 4, 0:D], ps[:, s + 1, 0:D], ACT.Copy)
                A.activation(rows[:, :, D], ps[:, s + 1, D:D + NREL], ACT.Copy).then_inc(rows_rdy, 1)
                A.activation(C1[:, b, 0:NREL], ps[:, s + 1, D + NREL:D + 2 * NREL], ACT.Copy).then_inc(pn_free, 1)
                pn[0] += 1
            act.wait_ge(pn_free, pn[0])
            join.to("rel_table")

            def onehotT(q, count):
                def body(t):
                    n = count(t)
                    act.wait_ge(q["turned"], n + 1)
                    if t.has(2):
                        act.wait_ge(q["node"], n - 1)
                    A.activation(ohT[:, t.h], ps[:, t.h, :].rearrange("p (j d) -> p j d", j=B), ACT.Copy).then_inc(q["onehotT"], 1)
                return body

            def rows_copied(n):
                def body(t):
                    act.wait_ge(qm["rows"], t.n + 1)
                    if t.late(2):
                        act.wait_ge(qm["scanned"], t.n - 1)
                    A.activation(tz[0:B * n, t.h, :], ps[0:B * n, 4 + t.h, 0:2 * P], ACT.Copy).then_inc(qm["rows_sb"], 1)
                return body

            run(act, [(0, stage_indices(qm, idx5)), (2, rows_copied(1))])
            join.to("rel_max")

            def rel_exp(t):
                act.wait_ge(qd["logits"], t.n + 1)
                A.activation(small3[:, t.s4, 2 * B:3 * B], small3[:, t.s4, 0:B], ACT.Exp).then_inc(qd["exp"], 1)

            run(act, [(0, onehotT(qd, lambda t: t.n)), (2, rel_exp)])
            join.to("rel_den")
            run(act, [(0, stage_indices(qr, idx5)), (0, onehotT(qr, lambda t: t.n))])
            act.wait_ge(elu_in, 1)
            A.activation(T3[0], T3[0], ACT.Exp).then_inc(elu_exp, 1)
            root()
            join.to("tr_masked")
            turned(T[0])
            turned(T[1])
            turned(T[2])
            join.to("tr_T")
            product(T[3], ACT.Copy, 0.0)
            join.to("tr_keysT")
            for b in range(NBLK):
                act.wait_ge(pn_full, pn[0] + 1)
                s = 2 * (pn[0] % 2)
                A.activation(Qn[:, b, :], ps[:, s, 0:D], ACT.Copy)
                A.activation(T3[4][:, b, :], ps[:, s, D:2 * D], ACT.Copy).then_inc(pn_free, 1)
                pn[0] += 1
            act.wait_ge(pn_free, pn[0])
            join.to("tr_values")

            def picked(t):
                act.wait_ge(qm["back"], t.n + 1)
                if t.late(4):
                    act.wait_ge(qm["sums"], t.n - 3)
                o = 128 * t.h
                A.activation(gm[:, t.s4, :, 0:NHEAD], ps[:, 6, o:o + B * NHEAD].rearrange("p (j g) -> p j g", j=B), ACT.Copy)
                A.activation(gm[:, t.s4, :, NHEAD:NHEAD + 1], ps[:, 6, o + 32:o + 32 + B * NHEAD].rearrange("p (j g) -> p j g", j=B)[:, :, 0:1],
                             ACT.Copy).then_inc(qm["picked"], 1)

            run(act, [(0, stage_indices(qm, idx5)), (2, rows_copied(NHEAD)), (3, picked), (0, onehotT(qm, lambda t: t.k))], 1)
            join.to("tr_zero")

            def tr_exp(t):
                act.wait_ge(qt["logits"], t.n + 1)
                if t.late(4):
                    act.wait_ge(qt["sums"], t.n - 3)
                A.activation(msg[:, t.s4, :, D:W2N], small3[:, t.s4, 0:B * NHEAD].rearrange("p (j g) -> p j g", j=B), ACT.Exp).then_inc(qt["exp"], 1)

            run(act, [(0, stage_indices(qt, idx1)), (2, tr_exp), (0, onehotT(qt, lambda t: t.n))])
            join.to("tr_mean")
            turned(T[1])
            join.to("tr_meanT")
            product(T[2], ACT.Identity, col[:, 0:1])
            join.to("tr_mixT")
            turned(T[3])
            join.to("tr_mix")
            root()
            join.to("tr_norm1")
            turned(T[1])
            join.to("tr_norm1T")
            hid = [T[2], T[3], T[4], AG[:, 0:NPAD]]
            for c in range(4):
                product(hid[c], ACT.Gelu, col[:, 1 + c:2 + c])
            join.to("tr_hiddenT")
            product(T[1], ACT.Identity, col[:, 5:6])
            join.to("tr_ffT")
            turned(T[3])
            join.to("tr_ff")
            root()
            root()
            join.to("mp_weights")
            turned(T[0])
            join.to("mp_T")
            turned(T[1])
            join.to("mp_table")
            run(act, [(0, stage_indices(qp, idx1)), (2, relu(qp)), (0, onehotT(qp, lambda t: t.n))])
            join.to("mp")
            turned(T[3])
            for g in range((NBLK + 3) // 4):
                n = min(4, NBLK - 4 * g) * P
                act.wait_ge(pn_full, pn[0] + 1)
                A.activation(T[4][0:1, g * 512:g * 512 + n], ps[0:1, 2 * (pn[0] % 2), 0:n], ACT.Copy).then_inc(pn_free, 1)
                pn[0] += 1
            act.wait_ge(pn_free, pn[0])
            join.to("mp_sumT")
            product(T[0], ACT.Copy, 0.0)
            join.to("mp_msgT")
            product(T[1], ACT.Relu, col[:, 0:1])
            join.to("mp_updT")
            turned(T[2])
            join.to("mp_upd")
            root()
            join.to("mp_out")

        @block.tensor
        def _(pe):
            join = Join(pe)
            M = nc.tensor
            pn = [0]

            def group():
                if pn[0] >= 2:
                    pe.wait_ge(pn_free, pn[0] - 1)
                pn[0] += 1
                return 2 * ((pn[0] - 1) % 2)

            def turn(src, cols=None):
                for g in range((NBLK + 3) // 4):
                    s = group()
                    for j in range(min(4, NBLK - 4 * g)):
                        o = ps[:, s, j * P:(j + 1) * P] if cols is None else ps[0:1, s, j * P:(j + 1) * P]
                        ins = M.transpose(o, src(4 * g + j), ident[:, :])
                    ins.then_inc(pn_full, 1)

            def turn_all(t):
                turn(lambda b: t[:, b, :])

            def product(*terms):
                for g in range(NG):
                    s = group()
                    for n, (w, x) in enumerate(terms):
                        ins = M.matmul(ps[:, s, 0:G], w, x[:, g * G:(g + 1) * G], start=(n == 0), stop=(n == len(terms) - 1))
                    ins.then_inc(pn_full, 1)

            def turned_back(t):
                turn(lambda b: t[:, b * P:(b + 1) * P])

            pe.wait_ge(cst, 6)
            pe.wait_ge(cnt_rdy, 1)
            M.matmul(ps[0:EP, 0, 0:NBLK], tri[0:EP, 0:EP], cnt[0:EP], start=True, stop=True)
            M.matmul(ps[:, 1, 0:NBLK], ones[0:EP, :], cnt[0:EP], start=True, stop=True).then_inc(cnt_ps, 1)
            join.to("records")

            def sums(q, w, out_of, ready="relu", rhs=None, taken=None):
                def body(t):
                    pe.wait_ge(q[ready], t.n + 1)
                    if taken:
                        if t.late(1):
                            pe.wait_ge(q[taken], t.n * 2)
                    elif t.late(2):
                        pe.wait_ge(q["acc"], t.n * B - B)
                    for j in range(B):
                        x = rhs(t, j) if rhs else msg[:, t.s4, j, 0:w]
                        ins = M.matmul(out_of(t, j), oh[:, t.s4, j, :], x, start=True, stop=True)
                    ins.then_inc(q["sums"], 1)
                return body

            def edge_terms(t):
                pe.wait_ge(qg.ea[t.h], t.i * 16 + 16)
                if t.late(2):
                    pe.wait_ge(qg["added"], t.n - 1)
                for j in range(B):
                    ins = M.matmul(ps[:, t.h, j * P:(j + 1) * P], ear[0:EA, t.h, j * P:(j + 1) * P], wt[0:EA, 0:D],
                                   start=True, stop=True)
                ins.then_inc(qg["edge"], 1)

            def keys_spread(t):
                pe.wait_ge(qs["keys"], t.n + 1)
                if t.late(2):
                    pe.wait_ge(rank_sem, t.n * 2 - 3)
                for j in range(B):
                    ins = M.transpose(ps[:, 6 + t.h, j * P:(j + 1) * P], small2[:, t.s4, j:j + 1].to_broadcast([P, P]), ident[:, :])
                ins.then_inc(qs["spread"], 1)

            def moved(t):
                pe.wait_ge(qs["perm"], t.n + 1)
                if t.late(1):
                    pe.wait_ge(qs["attr_sb"], t.n)
                    pe.wait_ge(qs["fields"], t.n)
                for j in range(B):
                    M.matmul(ps[0:EAB, 4, j * P:(j + 1) * P], recin[:, t.s4, j, 0:EAB], perm[:, t.h, j, :], start=True, stop=True)
                for j in range(B):
                    ins = M.matmul(ps[:, 5, t.h * 64 + 4 * j:t.h * 64 + 4 * j + 4], perm[:, t.h, j, :], recin[:, t.s4, j, EAB:REC],
                                   start=True, stop=True)
                ins.then_inc(qs["moved"], 1)

            seg_gine = sums(qg, D, lambda t, j: ps[:, 2 + t.h, j * P:(j + 1) * P])
            for l in range(3):
                join.to(f"weights{l}")
                if l == 0:
                    run(pe, [(0, keys_spread), (1, moved), (7, seg_gine), (5, edge_terms)], l)
                else:
                    run(pe, [(2, seg_gine), (0, edge_terms)], l)
                join.to(f"gine{l}")
                turn_all(XL)
                join.to(f"sumT{l}")
                product((wt[:, D:2 * D], T[1]))
                join.to(f"hiddenT{l}")
                product((wt[:, 2 * D:3 * D], T[2]))
                join.to(f"outT{l}")
                turned_back(T[3])
            join.to("rel_weights")
            turn_all(H)
            join.to("rel_T")
            for r in range(2 * NREL):
                c = 0 if r < NREL else 1
                ins = M.matmul(ps[:, 4, r:r + 1], T[1][:, r * D:(r + 1) * D], col[:, c:c + 1], start=True, stop=True)
            ins.then_inc(relv_ps, 1)
            join.to("rel_vectors")
            for b in range(NBLK):
                s = group()
                hb = T[0][:, b * P:(b + 1) * P]
                M.matmul(ps[:, s, :], hb, wt[:, 0:512], start=True, stop=True)
                M.matmul(ps[:, s + 1, 0:D + 2 * NREL], hb, wt[:, 512:NREL * D + 2 * NREL], start=True, stop=True).then_inc(pn_full, 1)
            join.to("rel_table")

            def turn_onehot(q, count):
                def body(t):
                    pe.wait_ge(q["onehot"], t.n + 1)
                    if t.has(2):
                        pe.wait_ge(q["onehotT"], count(t) - 1)
                    for j in range(B):
                        ins = M.transpose(ps[:, t.h, j * P:(j + 1) * P], oh[:, t.s4, j, :], ident[:, :])
                    ins.then_inc(q["turned"], 1)
                return body

            def turn_scores(n):
                def body(t):
                    pe.wait_ge(qm["scores"], t.n + 1)
                    if t.late(2):
                        pe.wait_ge(qm["rows_sb"], t.n - 1)
                    M.transpose(ps[0:B * n, 4 + t.h, 0:P], small3[:, t.s4, 0:B * n], ident[:, :])
                    M.transpose(ps[0:B * n, 4 + t.h, P:2 * P], small3[:, t.s4, 32:32 + B * n], ident[:, :]).then_inc(qm["rows"], 1)
                return body

            def turn_maxima(n):
                def body(t):
                    pe.wait_ge(qm["scanned"], t.n + 1)
                    if t.late(1):
                        pe.wait_ge(qm["picked"], t.n)
                    pe.sem_inc(pe_go, 1)
                    o, rows = 128 * t.h, B * n
                    M.transpose(ps[:, 6, o:o + rows], sf[0:rows, t.h, P:2 * P], ident[0:rows, 0:rows])
                    M.transpose(ps[:, 6, o + 32:o + 32 + rows], ne[0:rows, t.h, 1:P + 1], ident[0:rows, 0:rows]).then_inc(qm["back"], 1)
                return body

            def node_rows(q, rhs, out_of, count, free, local=False):
                def body(t):
                    pe.wait_ge(q["onehotT"], count(t) + 1)
                    if t.has(2):
                        pe.wait_ge(q[free], t.n - 1)
                    blocks = blocks_of(pe, PE, t)
                    for j in range(B):
                        ins = M.matmul(out_of(t, j), ohT[:, t.h, j, :], rhs(blocks[j]), start=True, stop=True)
                    ins.then_inc(q["node"], 1)
                return body

            def rows_at(v, w):
                return lambda b: v[:, bass.ds(b, 1), 0:w].rearrange("p a w -> p (a w)")

            own = lambda t: t.n
            run(pe, [(4, sums(qm, 0, lambda t, j: ps[:, 7, t.h * 64 + 10 * j:t.h * 64 + 10 * j + 10], ready="picked", taken="ch_acc",
                              rhs=lambda t, j: gm[:, t.s4, j, 0:10])),
                     (1, turn_scores(1)), (2, turn_maxima(1))])
            join.to("rel_max")
            run(pe, [(4, sums(qd, 0, lambda t, j: ps[:, 4 + t.h, j * NREL:(j + 1) * NREL], ready="weights",
                              rhs=lambda t, j: gm[:, t.s4, j, 0:NREL])),
                     (1, node_rows(qd, rows_at(C1, 2 * NREL), lambda t, j: ps[:, 2 + t.h, j * 2 * NREL:(j + 1) * 2 * NREL], own, "logits")),
                     (0, turn_onehot(qd, own))])
            join.to("rel_den")

            def pair(w):
                return lambda t, j: ps[:, 4 + 2 * t.h + j // 2, (j % 2) * 256:(j % 2) * 256 + w]

            run(pe, [(3, sums(qr, D, pair(D), ready="messages")),
                     (1, node_rows(qr, rows_at(C1, NREL), lambda t, j: ps[:, 2 + t.h, j * NREL:(j + 1) * NREL], own, "messages")),
                     (0, turn_onehot(qr, own))])
            join.to("tr_masked")
            turn_all(T3[3])
            turn_all(T3[4])
            turn_all(XL)
            join.to("tr_T")
            product(*[(WKb[:, t, :], T[t]) for t in range(NTYPE)])
            join.to("tr_keysT")
            for b in range(NBLK):
                s = group()
                for t in range(NTYPE):
                    ins = M.matmul(ps[:, s, 0:2 * D], T[t][:, b * P:(b + 1) * P], WQV[:, t, :], start=(t == 0), stop=(t == NTYPE - 1))
                ins.then_inc(pn_full, 1)
            join.to("tr_qv")
            for b in range(NBLK):
                kb, s = T[3][:, b * P:(b + 1) * P], 4 + 2 * (b % 2)
                if b >= 2:
                    pe.wait_ge(vals_rdy, 2 * (b - 1))
                M.matmul(ps[:, s, :], kb, WE[:, 0:512], start=True, stop=True).then_inc(kw_ps, 1)
                M.matmul(ps[:, s + 1, 0:D], kb, WE[:, 512:NREL * D], start=True, stop=True).then_inc(kw_ps, 1)
            join.to("tr_values")
            local = lambda t: t.k
            run(pe, [(4, sums(qm, 0, lambda t, j: ps[:, 7, t.h * 64 + 9 * j:t.h * 64 + 9 * j + 9], ready="picked", taken="ch_acc",
                              rhs=lambda t, j: gm[:, t.s4, j, 0:9])),
                     (1, node_rows(qm, rows_at(Qn, D), lambda t, j: ps[:, 2 + t.h, j * P:(j + 1) * P], local, "scores")),
                     (2, turn_scores(NHEAD)), (3, turn_maxima(NHEAD)), (0, turn_onehot(qm, local))], 1)
            join.to("tr_zero")
            run(pe, [(4, sums(qt, W2N, pair(W2N), ready="messages")),
                     (1, node_rows(qt, rows_at(MX, NHEAD), lambda t, j: ps[:, 2 + t.h, j * NHEAD:(j + 1) * NHEAD], own, "logits")),
                     (0, turn_onehot(qt, own))])
            join.to("tr_mean")
            turn_all(T3[0])
            join.to("tr_meanT")
            product((wt[:, 0:D], T[1]))
            join.to("tr_mixT")
            turned_back(T[2])
            join.to("tr_norm1")
            turn_all(T3[0])
            join.to("tr_norm1T")
            for c in range(4):
                product((wt[:, D + c * D:D + (c + 1) * D], T[1]))
            join.to("tr_hiddenT")
            hid = [T[2], T[3], T[4], AG[:, 0:NPAD]]
            product(*[(wt[:, D + FF + c * D:D + FF + (c + 1) * D], hid[c]) for c in range(4)])
            join.to("tr_ffT")
            turned_back(T[1])
            join.to("mp_weights")
            turn_all(H)
            join.to("mp_T")
            for g in range((NBLK + 3) // 4):
                s, n = group(), min(4, NBLK - 4 * g)
                for j in range(n):
                    hb = T[0][:, (4 * g + j) * P:(4 * g + j + 1) * P]
                    ins = M.matmul(ps[:, s, j * P:(j + 1) * P], hb, wt[:, D:2 * D], start=True, stop=True)
                ins.then_inc(pn_full, 1)
                if g >= 2:
                    pe.wait_ge(nt_free, g - 1)
                for j in range(n):
                    hb = T[0][:, (4 * g + j) * P:(4 * g + j + 1) * P]
                    ins = M.matmul(ps[:, 4 + g % 2, j * P:(j + 1) * P], hb, wt[:, 2 * D:3 * D], start=True, stop=True)
                ins.then_inc(nt_ps, 1)
            join.to("mp_table")

            def nd_mp(t):
                pe.wait_ge(qp["onehotT"], t.n + 1)
                pe.wait_ge(qp.ea[t.h], t.i * 16 + 16)
                if t.late(2):
                    pe.wait_ge(qp["added"], t.n - 1)
                blocks = blocks_of(pe, PE, t)
                for j in range(B):
                    o = ps[:, 2 + t.h, j * P:(j + 1) * P]
                    M.matmul(o, ear[:, t.h, j * P:(j + 1) * P], wt[:, 0:D], start=True, stop=False)
                    ins = M.matmul(o, ohT[:, t.h, j, :], rows_at(T3[2], D)(blocks[j]), start=False, stop=True)
                ins.then_inc(qp["node"], 1)

            run(pe, [(3, sums(qp, D + 1, pair(D + 1))), (1, nd_mp), (0, turn_onehot(qp, own))])
            join.to("mp")
            turn(lambda b: agg3[:, b, 0:D])
            turn(lambda b: agg3[:, b, D:D + 1], cols=1)
            join.to("mp_sumT")
            product((wt[:, 3 * D:4 * D], T[3]), (b2row[0:1, :], T[4][0:1]))
            join.to("mp_msgT")
            product((wt[:, 4 * D:5 * D], T[0]))
            join.to("mp_updT")
            turned_back(T[1])
            join.to("mp_out")


_INS = ["x", "src", "dst", "edge_attr_32", "edge_attr_64", "edge_type_5", "node_type_3",
        "L0_gnn_We", "L0_gnn_be", "L0_gnn_W1", "L0_gnn_b1", "L0_gnn_W2", "L0_gnn_b2", "L0_gnn_gamma", "L0_gnn_beta",
        "L1_gnn_WV", "L1_gnn_a_vec",
        "L2_gnn_W_Q", "L2_gnn_W_K", "L2_gnn_W_V", "L2_gnn_W_edge", "L2_gnn_mu", "L2_gnn_W_out", "L2_gnn_b_out",
        "L2_gnn_ln1_g", "L2_gnn_ln1_b", "L2_gnn_W1", "L2_gnn_b1", "L2_gnn_W2", "L2_gnn_b2", "L2_gnn_ln2_g", "L2_gnn_ln2_b",
        "L3_gnn_b1", "L3_gnn_b2", "L3_gnn_bu", "L3_gnn_gamma", "L3_gnn_beta"]
_TURNED = {"WKT": ("L1_gnn_WK", (0, 2, 1)), "WQT": ("L1_gnn_WQ", (0, 2, 1)), "W3T": ("L3_gnn_W1", (1, 0)),
           "W32T": ("L3_gnn_W2", (1, 0)), "WuT": ("L3_gnn_Wu", (1, 0))}


def kernel(**inputs):
    import concourse.bacc as _bacc
    from concourse.bass_utils import run_bass_kernel_spmd as _run

    nc = _bacc.Bacc("TRN2", target_bir_lowering=False, num_devices=1)
    arrays, args = {}, {}
    laid = {name: inputs[name] for name in _INS}
    laid.update({name: np.transpose(inputs[of], axes) for name, (of, axes) in _TURNED.items()})
    for name, v in laid.items():
        v = np.ascontiguousarray(v)
        arrays[f"in_{name}"] = v
        args[name] = nc.dram_tensor(f"in_{name}", v.shape, mybir.dt.from_np(v.dtype), kind="ExternalInput").ap()
    out = nc.dram_tensor("out_x", (N, D), F32, kind="ExternalOutput").ap()
    build(nc, args, out)
    r = _run(nc, [arrays], core_ids=[0])
    return r.results[0]["out_x"]
```

```python
from contextlib import ExitStack

import numpy as np

import concourse.bass as bass
from concourse import mybir

F32 = mybir.dt.float32
I32 = mybir.dt.int32
ALU = mybir.AluOpType
ACT = mybir.ActivationFunctionType
DVE, PE = mybir.EngineType.DVE, mybir.EngineType.PE
AX = mybir.AxisListType.X

P = 128
N, E, D = 3125, 50000, 128
NBLK = (N + P - 1) // P
NPAD = NBLK * P
LASTROWS = N - (NBLK - 1) * P
EA, EB = 64, 32
NREL, NTYPE, NHEAD = 5, 3, 8
HD = D // NHEAD
FF = 4 * D
EP, EC = 125, 400
B = 4
NT = -(-((E + NBLK * (P - 1)) // P) // (2 * B)) * 2 * B
NB = NT // B
REC = EA + EB + 4
SC = 8
FILL = 13
G = 400
NG = NPAD // G
T1W = D + 4
EAB = EA + EB
W2N = D + NHEAD
LN_EPS = 1e-5
BIG = 1e30


def build(nc, a, out):
    ctx = ExitStack()
    with ctx:
        def sb(name, shape, dt=F32):
            return ctx.enter_context(nc.sbuf_tensor(name, shape, dt))

        def sem(name):
            return ctx.enter_context(nc.semaphore(name))

        def dram(name, shape, dt=F32):
            return nc.dram_tensor(name, shape, dt, kind="Internal").ap()

        rec = dram("slot_records", [NT * P, REC])
        eat = dram("edge_attr_T", [NB, EAB, B * P])
        tab0 = dram("table_gine", [NPAD, D])
        tab1 = dram("table_rel", [NPAD * NREL, T1W])
        tab2k = dram("table_keys", [NPAD * NREL, D])
        tab2v = dram("table_values", [NPAD, D])
        tab3 = dram("table_msg", [NPAD, D])

        ident = sb("ident", [P, P])
        iota_n = sb("iota_n", [P, P])
        ones = sb("ones", [P, P])
        tri = sb("tri", [P, P])
        dl = sb("dl", [P, NT])
        et = sb("et", [P, NT])
        idx1 = sb("idx1", [P, NT + B], I32)
        idx5 = sb("idx5", [P, NT + B], I32)
        nb = sb("nb", [P, NT], I32)
        score = sb("score", [P, NT * NHEAD])
        X = sb("X", [P, NBLK, D])
        H = sb("H", [P, NBLK, D])
        AG = sb("AG", [P, NBLK * W2N])
        MX = sb("MX", [P, NBLK, NHEAD])
        C1 = sb("C1", [P, NBLK, 2 * NREL])
        arena = sb("arena", [P, 5 * NPAD])
        ring = sb("ring", [P, 4, B, T1W])
        idxr = sb("idxr", [P, 4, B], I32)
        oh = sb("oh", [P, 4, B, P])
        ohT = sb("ohT", [P, 2, B, P])
        mraw = sb("mraw", [P, 2, B, P])
        msg = sb("msg", [P, 4, B, W2N])
        ear = sb("ear", [P, 2, B * P])
        small = sb("small", [P, 4, 64])
        small2 = sb("small2", [P, 4, 64])
        small3 = sb("small3", [P, 4, 64])
        small4 = sb("small4", [P, 4, 64])
        gm = sb("gm", [P, 4, B, 10])
        tz = sb("tz", [B * NHEAD, 2, 2 * P])
        ne = sb("ne", [B * NHEAD, 2, P + 1])
        sf = sb("sf", [B * NHEAD, 2, 2 * P])
        stat = sb("stat", [P, 4, 32])
        lnst = sb("lnst", [P, NBLK, 6])
        pcol = sb("pcol", [P, 2])
        wt = sb("wt", [P, 1300])
        bc = sb("bc", [P, 3, D])
        col = sb("col", [P, 16])
        b2row = sb("b2row", [1, D])

        ps = ctx.enter_context(nc.psum_tensor("ps", [P, 8, 512], F32))

        aren = arena[:, :]
        T = [aren[:, i * NPAD:(i + 1) * NPAD] for i in range(5)]


        slotr = sb("slotr", [P, 2, SC], I32)

        joined = sem("joined")
        dve_ch = sem("dve_chain")
        pn_full, pn_free = sem("node_psum_full"), sem("node_psum_free")
        ln_var, ln_std = sem("variance_ready"), sem("deviation_ready")
        w_in = sem("weights_in")
        t_out = sem("table_out")
        pool_go, act_go, pe_go = (sem(f"{e}_waits_passed") for e in ("pool", "act", "pe"))
        rows_rdy, vals_rdy = sem("rel_rows_ready"), sem("key_rows_ready")
        rows_out = [sem(f"rel_rows_out{h}") for h in range(2)]
        keys_out = [sem(f"key_rows_out{h}") for h in range(2)]
        rows_ch = sem("records_chain")
        rank_sem, trs_sem = sem("places_chain"), sem("tr_score_chain")
        x_pad = sem("x_padding")
        bn_done = sem("feature_statistics")
        types_set, onehot_tr = sem("types_set"), sem("onehot_for_turning")
        relv_ps = sem("rel_vectors_in_psum")
        elu_in, elu_exp = sem("elu_input"), sem("elu_exp")
        kw_ps = sem("key_rows_in_psum")
        nt_ps, nt_free = sem("node_terms_in_psum"), sem("node_terms_taken")

        STAGES = (["slots", "records"]
                  + [f"{n}{l}" for l in range(3) for n in ("weights", "gine", "sumT", "hiddenT", "outT", "out", "norm")]
                  + ["rel_weights", "rel_T", "rel_vectors", "rel_table", "relA", "rel_max", "relD", "rel_den", "relB",
                     "rel_out"]
                  + ["tr_clear", "tr_weights", "tr_masked", "tr_T", "tr_keysT", "tr_qv", "tr_keys", "tr_values",
                     "trA", "tr_zero", "trB", "tr_mean", "tr_meanT", "tr_mixT", "tr_mix", "tr_norm1", "tr_norm1T",
                     "tr_hiddenT", "tr_ffT", "tr_ff", "tr_out"]
                  + ["mp_weights", "mp_T", "mp_node", "mp_table", "mp", "mp_sumT", "mp_msgT", "mp_updT", "mp_upd",
                     "mp_out"])

        class Join:
            def __init__(self, eng):
                self.eng, self.n = eng, 0

            def to(self, stage):
                upto = STAGES.index(stage) + 1
                assert upto > self.n, stage
                while self.n < upto:
                    self.n += 1
                    self.eng.drain()
                    self.eng.sem_inc(joined, 1)
                    self.eng.wait_ge(joined, 5 * self.n)

        class Chain:
            def __init__(self, eng, s):
                self.eng, self.s, self.n, self.base = eng, s, 0, 0

            def __call__(self, ins):
                self.n += 1
                ins.then_inc(self.s, 1)
                self.eng.wait_ge(self.s, self.base + self.n)

            def loop(self, start, stop, body, step=1):
                n0 = self.base + self.n
                self.base, self.n = n0, 0
                body(start)
                per = self.n
                with self.eng.Fori(start + step, stop, step) as i:
                    self.base, self.n = (i - start) * (per // step) + n0, 0
                    body(i)
                    assert self.n == per
                self.base, self.n = n0 + per * ((stop - start) // step), 0

        class Steps:
            def __init__(self, eng, s, per):
                self.eng, self.s, self.per, self.m = eng, s, per, per

            def start(self, n):
                assert self.m == self.per, (self.m, self.per)
                self.base, self.m = n * self.per, 0

            def step(self, ins):
                self.m += 1
                ins.then_inc(self.s, 1)

            def done(self):
                self.eng.wait_ge(self.s, self.base + self.m)

        class Batch:
            def __init__(self, r, s, of=0):
                self.r, self.s, self.of = r, s, of
                self.k = r * 4 + s
                self.n = r * 4 + (s + of * NB)
                self.h, self.s4 = s % 2, s % 4
                self.i = r * 2 + (s // 2 + of * (NB // 2))
                self.u = r + (s // 4 + of * (NB // 4))

            def back(self, lag):
                return Batch(self.r, self.s - lag, self.of)

            def has(self, lag):
                return not isinstance(self.k, int) or self.k >= lag

            def real(self):
                return not isinstance(self.k, int) or 0 <= self.k < NB

            def late(self, lag):
                return not isinstance(self.n, int) or self.n >= lag

        def run(eng, stages, of=0):
            deep = max(lag for lag, _ in stages)
            lead = -(-deep // 4) + 1

            def turn(r, s):
                parts = [body(t) for lag, body in stages for t in [Batch(r, s, of).back(lag)] if t.real()]
                parts = [part for part in parts if part is not None]
                while parts:
                    parts = [part for part in parts if next(part, "ended") != "ended"]
            for k in range(4 * lead):
                turn(k // 4, k % 4)
            with eng.Fori(lead, NB // 4) as r:
                for s in range(4):
                    turn(r, s)
            for k in range(NB, NB + deep):
                turn(k // 4, k % 4)

        def halves(eng, body, n):
            for i in range(2):
                for h in range(2):
                    body(i, h, 2 * i + h)
            with eng.Fori(2, n // 2) as i:
                for h in range(2):
                    body(i, h, i * 2 + h)

        def late(k, n):
            return not isinstance(k, int) or k >= n

        def blocks_of(eng, which, t):
            _, values = nc.values_load_multi_w_load_instructions(
                nb[0:1, bass.ds(t.k * B, B)], engines=[which], min_val=0, max_val=NBLK - 1,
                skip_runtime_bounds_check_because="nb counts the blocks that end at or before a tile, cut at NBLK - 1")
            return values

        class Sems:
            def __init__(self, p, *names, gath=False, ea=False):
                self.of = {n: sem(f"{p}_{n}") for n in names}
                self.gath = [sem(f"{p}_gathered{h}") for h in range(4)] if gath else None
                self.ea = [sem(f"{p}_attr_in{h}") for h in range(2)] if ea else None

            def __getitem__(self, name):
                return self.of[name]

        qg = Sems("gine", "index", "edge", "onehot", "added", "relu", "sums", "acc", gath=True, ea=True)
        qm = Sems("max", "index", "onehot", "turned", "onehotT", "node", "scores", "rows", "rows_sb", "scanned",
                  "back", "picked", "sums", "acc", "ch_score", "ch_scan", "ch_acc", gath=True)
        qd = Sems("relD", "onehot", "onehot_t", "turned", "onehotT", "node", "logits", "exp", "weights", "sums", "acc", "chain",
                  "chain2")
        qr = Sems("relB", "index", "onehot", "turned", "onehotT", "node", "messages", "sums", "acc", "chain", gath=True)
        qt = Sems("trB", "index", "onehot", "turned", "onehotT", "node", "logits", "exp", "messages", "sums", "acc",
                  gath=True)
        qp = Sems("mp", "index", "onehot", "turned", "onehotT", "node", "added", "relu", "sums", "acc", gath=True, ea=True)
        qs = Sems("sort", "chain", "keys", "spread", "perm", "moved", "attr_sb", "fields")
        fill_out, cst, cst2 = sem("records_filled"), sem("constants"), sem("index_constants")
        el_in = sem("edge_list_in")
        cnt_rdy, cnt_ps = sem("counts_ready"), sem("counts_in_psum")
        att_in = [sem(f"attr_rows_in{h}") for h in range(2)]
        rec_rdy = sem("records_built")
        scat = [sem(f"records_scattered{h}") for h in range(2)]
        rin = [sem(f"records_in{h}") for h in range(4)]
        rout = [sem(f"attr_T_out{h}") for h in range(2)]
        fin = sem("result_out")

        cum = aren[0:EP, 0:NBLK * EC].rearrange("p (b c) -> p b c", b=NBLK)

        def spare(n, rows=EP):
            return aren[0:rows, NBLK * EC + n * EC:NBLK * EC + (n + 1) * EC]

        dsti, srci, eti, bki, slot = (spare(n).bitcast(I32) for n in (0, 1, 2, 3, 10))
        bkf, dstf, mask, zero, slotf, tmp = (spare(n) for n in (4, 5, 6, 7, 8, 9))
        fields = AG[0:EP, 0:4 * EC].rearrange("p (c f) -> p c f", f=4)
        iota_t, nbf = score[:, 0:NT], score[:, NT:2 * NT]
        recb = T[2][0:EP, 0:2 * SC * REC].rearrange("p (h c r) -> p h c r", h=2, c=SC)
        recin = T[3][:, 0:4 * B * REC].rearrange("p (h c r) -> p h c r", h=4, c=B)
        fillb = msg[:, :, :, :].rearrange("p a b d -> p (a b d)")[:, 0:FILL * REC].rearrange("p (s r) -> p s r", r=REC)
        keyT = T[4][:, 0:2 * B * P].rearrange("p (h b d) -> p h b d", h=2, b=B)
        perm = T[4][:, 2 * B * P:4 * B * P].rearrange("p (h b d) -> p h b d", h=2, b=B)
        eato = T[1][0:EAB, 0:2 * B * P].rearrange("p (h c) -> p h c", h=2)
        iota_p, iota_pi = pcol[:, 0:1], pcol[:, 1:2].bitcast(I32)
        cnt, prefix, tot, nt_f = (stat[:, q, 0:NBLK] for q in range(4))
        wend, wst, off = (small[:, 0, 0:NBLK], small[:, 1, 0:NBLK], small3[:, 0, 0:NBLK])
        nt_i = small2[:, 0, 0:NBLK].bitcast(I32)
        SK, PW = score[:, 0:NT], score[:, NT:2 * NT]
        XL = AG[:, 0:NPAD].rearrange("p (b d) -> p b d", b=NBLK)
        Qn = XL
        agg2 = AG[:, :].rearrange("p (b w) -> p b w", b=NBLK)
        agg3 = AG[:, 0:NBLK * (D + 1)].rearrange("p (b w) -> p b w", b=NBLK)
        DEN = MX[:, :, 0:NREL]
        T3 = [t.rearrange("p (b d) -> p b d", b=NBLK) for t in T]
        WK_o, WE = 768, score[:, 0:NREL * D]
        WQV = wt[:, 0:NTYPE * 2 * D].rearrange("p (t c) -> p t c", t=NTYPE)
        WKb = wt[:, WK_o:WK_o + NTYPE * D].rearrange("p (t c) -> p t c", t=NTYPE)
        WEb = WE.rearrange("p (t c) -> p t c", t=NREL)
        ntype_i = small2[:, 1, 0:NBLK].bitcast(I32)
        ntype_f = small3[:, 1, 0:NBLK]
        muv = small[:, 0, 0:NHEAD * NREL]
        ohx = T[0][:, 0:2 * B * P].rearrange("p (h b d) -> p h b d", h=2, b=B)
        kwb = T[0][:, 0:2 * NREL * D].rearrange("p (h c) -> p h c", h=2)

        def per_block(v):
            return v.unsqueeze(2).to_broadcast([P, NBLK, D])

        def per_feature(v):
            return v.unsqueeze(1).to_broadcast([P, NBLK, D])

        block = ctx.enter_context(nc.Block())

        @block.sync
        def _(sp):
            join = Join(sp)
            w = [0]

            def load(dst, src, **how):
                w[0] += 16
                sp.dma_start(dst, src, **how).then_inc(w_in, 16)

            def landed():
                sp.wait_ge(w_in, w[0])

            def rowbc(q, src):
                load(bc[:, q, :], src.rearrange("(a d) -> a d", a=1).to_broadcast([P, D]))

            def column(j, src):
                load(col[:, j:j + 1], src.rearrange("(d a) -> d a", a=1))

            def table(tab, src, n):
                sp.dma_start(tab.rearrange("(b p) d -> p b d", p=P), src).then_inc(t_out, 16)
                sp.wait_ge(t_out, 16 * n)

            sp.dma_start(dsti, a["dst"].rearrange("(p c) -> p c", p=EP)).then_inc(el_in, 16)
            sp.dma_start(srci, a["src"].rearrange("(p c) -> p c", p=EP)).then_inc(el_in, 16)
            sp.dma_start(eti, a["edge_type_5"].rearrange("(p c) -> p c", p=EP)).then_inc(el_in, 16)
            sp.wait_ge(x_pad, 1)
            load(X[:, 0:NBLK - 1, :], a["x"][0:(NBLK - 1) * P, :].rearrange("(b p) d -> p b d", p=P))
            load(X[0:LASTROWS, NBLK - 1, :], a["x"][(NBLK - 1) * P:N, :])
            rowbc(2, a["L0_gnn_be"][0])
            landed()
            sp.wait_ge(cst2, 3)
            rv = rec.rearrange("(g p s) r -> g p s r", p=P, s=FILL)
            for g in range(NT // FILL):
                sp.dma_start(rv[g], fillb).then_inc(fill_out, 16)
            sp.wait_ge(fill_out, 16 * (NT // FILL))
            sp.wait_ge(el_in, 48)
            join.to("slots")
            e64 = a["edge_attr_64"].rearrange("(p c) d -> p c d", p=EP)
            e32 = a["edge_attr_32"].rearrange("(p c) d -> p c d", p=EP)

            def rows_in(i, h, k):
                if late(k, 2):
                    sp.wait_ge(scat[h], i * (16 * SC))
                sp.dma_start(recb[:, h, :, 0:EA], e64[:, bass.ds(k * SC, SC), :]).then_inc(att_in[h], 16)
                sp.dma_start(recb[:, h, :, EA:EA + EB], e32[:, bass.ds(k * SC, SC), :]).then_inc(att_in[h], 16)
            halves(sp, rows_in, EC // SC)
            for h in range(2):
                sp.wait_ge(scat[h], 16 * SC * (EC // SC // 2))
            join.to("records")
            rt = rec.rearrange("(t p) r -> p t r", p=P)
            for l in range(3):
                load(wt[0:EA, 0:D], a["L0_gnn_We"][l])
                load(wt[:, D:2 * D], a["L0_gnn_W1"][l])
                load(wt[:, 2 * D:3 * D], a["L0_gnn_W2"][l])
                column(0, a["L0_gnn_b1"][l])
                column(1, a["L0_gnn_b2"][l])
                rowbc(0, a["L0_gnn_gamma"][l])
                rowbc(1, a["L0_gnn_beta"][l])
                if l < 2:
                    rowbc(2, a["L0_gnn_be"][l + 1])
                landed()
                table(tab0, T3[0], l + 1)
                join.to(f"weights{l}")

                def slots_in(t):
                    if t.late(4):
                        sp.wait_ge(qs["moved"], t.n - 3)
                    sp.dma_start(recin[:, t.s4], rt[:, bass.ds(t.k * B, B), :]).then_inc(rin[t.s4], 16)

                def attrs(t):
                    if t.late(2):
                        sp.wait_ge(qg["edge"], t.n - 1)
                    if l == 0:
                        sp.wait_ge(rout[t.h], t.i * 16 + 16)
                    sp.dma_start(ear[0:EA, t.h, :], eat[bass.ds(t.k, 1), 0:EA, :].rearrange("a p c -> p (a c)")).then_inc(qg.ea[t.h], 16)
                run(sp, [(0, slots_in), (5, attrs)] if l == 0 else [(0, attrs)], l)
                join.to(f"norm{l}")
            for r in range(NREL):
                load(wt[:, r * D:(r + 1) * D], a["L1_gnn_WV"][r])
                load(T[1][:, r * D:(r + 1) * D], a["WKT"][r])
                load(T[1][:, (NREL + r) * D:(NREL + r + 1) * D], a["WQT"][r])
            column(0, a["L1_gnn_a_vec"][D:2 * D])
            column(1, a["L1_gnn_a_vec"][0:D])
            landed()
            join.to("rel_vectors")
            t1v = tab1.rearrange("(b p r) w -> b p (r w)", p=P, r=NREL)
            for b in range(NBLK):
                sp.wait_ge(rows_rdy, 2 * (b + 1))
                sp.dma_start(t1v[b], T[2 + b % 2][:, 0:NREL * T1W]).then_inc(rows_out[b % 2], 16)
            sp.wait_ge(rows_out[0], 16 * 13)
            sp.wait_ge(rows_out[1], 16 * 12)
            join.to("tr_clear")
            for h in range(NHEAD):
                s = slice(h * HD, (h + 1) * HD)
                load(WQV[s, :, h * HD:(h + 1) * HD], a["L2_gnn_W_Q"][:, h].rearrange("t d f -> d t f"))
                load(WQV[s, :, D + h * HD:D + (h + 1) * HD], a["L2_gnn_W_V"][:, h].rearrange("t d f -> d t f"))
                load(WKb[s, :, s], a["L2_gnn_W_K"][:, h].rearrange("t d f -> d t f"))
                load(WEb[s, :, s], a["L2_gnn_W_edge"][:, h].rearrange("t d f -> d t f"))
            load(muv, a["L2_gnn_mu"].rearrange("h r -> (h r)").rearrange("(a c) -> a c", a=1).to_broadcast([P, NHEAD * NREL]))
            load(ntype_i[:, 0:NBLK - 1], a["node_type_3"][0:(NBLK - 1) * P].rearrange("(b p) -> p b", p=P),
                 allow_slow_non_contiguous=True)
            load(ntype_i[0:LASTROWS, NBLK - 1:NBLK], a["node_type_3"][(NBLK - 1) * P:N].rearrange("(p a) -> p a", a=1))
            landed()
            join.to("tr_qv")
            t2v = tab2k.rearrange("(b p r) w -> b p (r w)", p=P, r=NREL)
            for b in range(NBLK):
                sp.wait_ge(vals_rdy, 2 * (b + 1))
                sp.dma_start(t2v[b], kwb[:, b % 2, :]).then_inc(keys_out[b % 2], 16)
            sp.wait_ge(keys_out[0], 16 * 13)
            sp.wait_ge(keys_out[1], 16 * 12)
            table(tab2v, T3[4], 4)
            join.to("trB")
            load(wt[:, 0:D], a["L2_gnn_W_out"])
            load(wt[:, D:D + FF], a["L2_gnn_W1"])
            load(wt[:, D + FF:D + 2 * FF].rearrange("p (c n) -> p c n", c=4), a["L2_gnn_W2"].rearrange("(c p) n -> p c n", p=P))
            column(0, a["L2_gnn_b_out"])
            for c in range(4):
                column(1 + c, a["L2_gnn_b1"][c * P:(c + 1) * P])
            column(5, a["L2_gnn_b2"])
            rowbc(0, a["L2_gnn_ln1_g"])
            rowbc(1, a["L2_gnn_ln1_b"])
            landed()
            join.to("tr_norm1")
            rowbc(0, a["L2_gnn_ln2_g"])
            rowbc(1, a["L2_gnn_ln2_b"])
            landed()
            join.to("tr_out")
            load(wt[0:EB, 0:D], a["W3T"][2 * D:2 * D + EB, :])
            load(wt[:, D:2 * D], a["W3T"][0:D, :])
            load(wt[:, 2 * D:3 * D], a["W3T"][D:2 * D, :])
            load(wt[:, 3 * D:4 * D], a["W32T"])
            load(wt[:, 4 * D:5 * D], a["WuT"])
            column(0, a["L3_gnn_bu"])
            load(b2row[:, :], a["L3_gnn_b2"].rearrange("(a d) -> a d", a=1))
            rowbc(0, a["L3_gnn_gamma"])
            rowbc(1, a["L3_gnn_beta"])
            rowbc(2, a["L3_gnn_b1"])
            landed()
            join.to("mp_node")
            table(tab3, T3[1], 5)
            join.to("mp_table")

            def attrs3(t):
                if t.late(2):
                    sp.wait_ge(qp["node"], t.n - 1)
                sp.dma_start(ear[0:EB, t.h, :], eat[bass.ds(t.k, 1), EA:EAB, :].rearrange("a p c -> p (a c)")).then_inc(qp.ea[t.h], 16)
            run(sp, [(0, attrs3)])
            join.to("mp_out")
            ov = out[0:(NBLK - 1) * P, :].rearrange("(b p) d -> p b d", p=P)
            sp.dma_start(ov, X[:, 0:NBLK - 1, :]).then_inc(fin, 16)
            sp.dma_start(out[(NBLK - 1) * P:N, :], X[0:LASTROWS, NBLK - 1, :]).then_inc(fin, 16)
            sp.wait_ge(fin, 32)

        @block.gpsimd
        def _(pool):
            join = Join(pool)
            pool.memset(ones[:, :], 1.0).then_inc(cst, 1)
            pool.iota(idx5[:, 0:NT], pattern=[[1, NT]], base=0, channel_multiplier=0).then_inc(cst, 1)
            pool.memset(ident[:, :], 0.0).then_inc(cst, 1)
            pool.memset(tri[:, :], 1.0).then_inc(cst, 1)
            pool.memset(fillb, 0.0).then_inc(cst2, 1)
            pool.wait_ge(cst2, 1)
            pool.memset(fillb[:, :, EA + EB + 1:EA + EB + 2], -1.0).then_inc(cst2, 1)
            pool.iota(iota_pi, pattern=[[0, 1]], base=0, channel_multiplier=1).then_inc(cst2, 1)
            pool.wait_ge(cst, 4)
            pool.affine_select(out=ident[:, :], in_=ident[:, :], compare_op=ALU.not_equal, fill=1.0, base=0,
                               pattern=[[-1, P]], channel_multiplier=1).then_inc(cst, 1)
            pool.affine_select(out=tri[:, :], in_=tri[:, :], compare_op=ALU.is_gt, fill=0.0, base=0,
                               pattern=[[1, P]], channel_multiplier=-1).then_inc(cst, 1)
            join.to("slots")

            def scatter(i, h, k):
                pool.wait_ge(rec_rdy, k + 1)
                pool.sem_inc(pool_go, 1)
                for c in range(SC):
                    pool.indirect_dma_start(
                        out=rec[:, :], out_offset=bass.IndirectOffsetOnAxis(ap=slotr[0:EP, h, c:c + 1], axis=0),
                        in_=recb[:, h, c, :], in_offset=None).then_inc(scat[h], 16)
            halves(pool, scatter, EC // SC)

            def gathers(q, free, table, width, of=0):
                def body(t):
                    pool.wait_ge(q["index"], t.n + 1)
                    if t.late(4):
                        pool.wait_ge(q[free], t.n - 3)
                    pool.sem_inc(pool_go, 1)
                    for j in range(B):
                        pool.indirect_dma_start(
                            out=ring[:, t.s4, j, 0:width], out_offset=None, in_=table[:, :],
                            in_offset=bass.IndirectOffsetOnAxis(ap=idxr[:, t.s4, j:j + 1], axis=0)).then_inc(q.gath[t.s4], 16)
                run(pool, [(0, body)], of)

            for l in range(3):
                join.to(f"weights{l}")
                gathers(qg, "added", tab0, D, l)
            join.to("rel_table")
            gathers(qm, "scores", tab1, T1W)
            join.to("rel_den")
            gathers(qr, "messages", tab1, T1W)
            join.to("tr_values")
            gathers(qm, "scores", tab2k, D, 1)
            join.to("tr_zero")
            gathers(qt, "messages", tab2v, D)
            join.to("mp_table")
            gathers(qp, "added", tab3, D)
            join.to("mp_out")

        @block.vector
        def _(dve):
            join = Join(dve)
            ch = Chain(dve, dve_ch)
            V = nc.vector
            norms = [0]

            def tt(o, x, y, op):
                return V.tensor_tensor(o, x, y, op)

            def norm(src, dst, relu=False, gb=False):
                for b in range(NBLK):
                    V.bn_stats(lnst[:, b, :], src[:, b, :]).then_inc(bn_done, 1)
                dve.wait_ge(bn_done, NBLK * (norms[0] + 1))
                m0, v0, m1, v1 = (lnst[:, :, c] for c in (1, 2, 4, 5))
                mean, var, gap = (stat[:, q, 0:NBLK] for q in (0, 1, 2))
                ch(tt(mean, m0, m1, ALU.add))
                ch(tt(gap, m0, m1, ALU.subtract))
                ch(tt(var, v0, v1, ALU.add))
                ch(tt(gap, gap, gap, ALU.mult))
                ch(V.tensor_scalar(mean, mean, 0.5, None, ALU.mult))
                ch(V.scalar_tensor_tensor(var, gap, D / 4, var, ALU.mult, ALU.add))
                ch(V.tensor_scalar(var, var, 1.0 / D, LN_EPS, ALU.mult, ALU.add))
                ch(tt(dst, src, per_block(mean), ALU.subtract))
                norms[0] += 1
                dve.sem_inc(ln_var, 1)
                dve.wait_ge(ln_std, norms[0])
                ch(V.reciprocal(stat[:, 3, 0:NBLK], stat[:, 2, 0:NBLK]))
                if relu:
                    ch(V.scalar_tensor_tensor(dst, dst, 0.0, per_block(stat[:, 3, 0:NBLK]), ALU.max, ALU.mult))
                else:
                    ch(tt(dst, dst, per_block(stat[:, 3, 0:NBLK]), ALU.mult))
                if gb:
                    ch(tt(dst, dst, per_feature(bc[:, 0, :]), ALU.mult))
                    ch(tt(dst, dst, per_feature(bc[:, 1, :]), ALU.add))

            dve.wait_ge(cst, 6)
            dve.wait_ge(cst2, 3)
            ch(V.tensor_copy(iota_p, iota_pi))
            ch(V.tensor_copy(iota_t, idx5[:, 0:NT]))
            ch(V.tensor_copy(iota_n[:, :], idx5[:, 0:P]))
            ch(V.memset(X[:, NBLK - 1, :], 0.0))
            dve.sem_inc(x_pad, 1)
            ch(V.memset(ne[:, :, :], 1.0))
            ch(V.memset(zero, 0.0))
            ch(V.memset(slotf, 0.0))
            ch(V.memset(nbf, 0.0))
            ch(V.memset(idx1[:, :], 0))
            ch(V.memset(idx5[:, :], 0))
            dve.wait_ge(el_in, 48)
            ch(V.tensor_single_scalar(bki, dsti, 7, ALU.arith_shift_right))
            ch(V.tensor_copy(bkf, bki))
            ch(V.tensor_copy(dstf, dsti))
            ch(V.tensor_copy(fields[:, :, 0], srci))
            ch(V.scalar_tensor_tensor(fields[:, :, 1], bkf, -float(P), dstf, ALU.mult, ALU.add))
            ch(V.tensor_copy(fields[:, :, 2], eti))
            ch(V.scalar_tensor_tensor(fields[:, :, 3], fields[:, :, 0], float(NREL), fields[:, :, 2], ALU.mult, ALU.add))

            def count(b):
                ch(V.tensor_scalar(mask, bkf, iota_n[0:EP, bass.ds(b, 1)], None, ALU.is_equal))
                ch(V.tensor_tensor_scan(tmp, mask, zero, 0.0, ALU.add, ALU.add))
                ch(V.tensor_scalar(cum[:, bass.ds(b, 1), :].rearrange("p a c -> p (a c)"), tmp, 0.0, None, ALU.add))
                ch(V.tensor_scalar(cnt[0:EP, bass.ds(b, 1)], tmp[:, EC - 1:EC], 0.0, None, ALU.add))
            ch.loop(0, NBLK, count)
            dve.sem_inc(cnt_rdy, 1)
            dve.wait_ge(cnt_ps, 1)
            ch(V.tensor_copy(prefix[0:EP], ps[0:EP, 0, 0:NBLK]))
            ch(V.tensor_scalar(tot, ps[:, 1, 0:NBLK], float(P - 1), None, ALU.add))
            ch(V.tensor_copy(nt_i, tot))
            ch(V.tensor_single_scalar(nt_i, nt_i, 7, ALU.arith_shift_right))
            ch(V.tensor_copy(nt_f, nt_i))
            ch(V.memset(off, 0.0))
            ch(V.tensor_tensor_scan(wend, nt_f, off, 0.0, ALU.add, ALU.add))
            ch(tt(wst, wend, nt_f, ALU.subtract))
            ch(V.tensor_scalar(off[0:EP], wst[0:EP], float(P), -1.0, ALU.mult, ALU.add))
            ch(tt(off[0:EP], off[0:EP], prefix[0:EP], ALU.add))

            def place(b):
                ch(V.tensor_scalar(mask, bkf, iota_n[0:EP, bass.ds(b, 1)], None, ALU.is_equal))
                ch(V.scalar_tensor_tensor(tmp, cum[:, bass.ds(b, 1), :].rearrange("p a c -> p (a c)"),
                                          off[0:EP, bass.ds(b, 1)], mask, ALU.add, ALU.mult))
                ch(tt(slotf, slotf, tmp, ALU.add))
                ch(V.scalar_tensor_tensor(nbf, iota_t, wend[:, bass.ds(b, 1)], nbf, ALU.is_ge, ALU.add))
            ch.loop(0, NBLK, place)
            ch(V.tensor_copy(slot, slotf))
            ch(V.tensor_scalar(nbf, nbf, float(NBLK - 1), None, ALU.min))
            ch(V.tensor_copy(nb[:, :], nbf))
            join.to("slots")

            def build_rows(i, h, k):
                dve.wait_ge(att_in[h], i * 32 + 32)
                if late(k, 2):
                    dve.wait_ge(scat[h], i * (16 * SC))
                V.tensor_scalar(slotr[0:EP, h, :], slot[:, bass.ds(k * SC, SC)], 0.0, None, ALU.add).then_inc(rows_ch, 1)
                V.tensor_scalar(recb[:, h, :, EA + EB:REC], fields[:, bass.ds(k * SC, SC), :], 0.0, None,
                                ALU.add).then_inc(rows_ch, 1)
                dve.wait_ge(rows_ch, k * 2 + 2)
                dve.sem_inc(rec_rdy, 1)
            halves(dve, build_rows, EC // SC)
            norm(X[:, :, :], H[:, :, :], relu=True)
            ch(tt(T3[0], H[:, :, :], per_feature(bc[:, 2, :]), ALU.add))
            join.to("records")
            ch(V.tensor_copy(XL, H[:, :, :]))


            def onehot(made, used, buf, t, count):
                depth = buf.shape[1]
                n = count(t)
                if late(n, depth):
                    dve.wait_ge(used, n - (depth - 1))
                if made is qg["onehot"] and t.of == 0:
                    dve.wait_ge(qs["fields"], t.n * 4 + 4)
                tt(buf[:, t.s4 % depth], iota_n[:, :].unsqueeze(1).to_broadcast([P, B, P]),
                   dl[:, bass.ds(t.k * B, B)].unsqueeze(2).to_broadcast([P, B, P]), ALU.is_equal).then_inc(made, 1)

            def onehots(made, used, buf, count=lambda t: t.n):
                def body(t):
                    for _ in range(3):
                        yield
                    onehot(made, used, buf, t, count)
                return body

            def accumulate(q, t, dst, src, op=ALU.add):
                blocks = blocks_of(dve, DVE, t)
                for j in range(B):
                    if t.late(1) or j:
                        dve.wait_ge(q["acc"], t.n * B + j)
                    o = dst(blocks[j])
                    tt(o, o, src(j), op).then_inc(q["acc"], 1)
                    yield

            def into(agg, w):
                return lambda b: agg[:, bass.ds(b, 1), 0:w].rearrange("p a w -> p (a w)")

            def flat(v):
                return v.rearrange("p j d -> p (j d)")

            sort = Steps(dve, qs["chain"], 2)

            def sort_keys(t):
                sort.start(t.n)
                dve.wait_ge(rin[t.s4], t.u * 16 + 16)
                f = recin[:, t.s4]
                key = small2[:, t.s4, 0:B]
                if t.late(4):
                    dve.wait_ge(qs["spread"], t.n - 3)
                sort.step(V.scalar_tensor_tensor(key, f[:, :, EAB + 1], 8.0, f[:, :, EAB + 2], ALU.mult, ALU.add))
                yield
                sort.done()
                sort.step(V.tensor_scalar(key, key, float(P), iota_p, ALU.mult, ALU.add))
                yield
                sort.done()
                dve.sem_inc(qs["keys"], 1)

            def sort_places(t):
                dve.wait_ge(qs["spread"], t.n + 1)
                tt(keyT[:, t.h], ps[:, 6 + t.h, :].rearrange("p (j d) -> p j d", j=B),
                   small2[:, t.s4, 0:B].unsqueeze(2).to_broadcast([P, B, P]), ALU.is_lt).then_inc(rank_sem, 1)
                yield
                dve.wait_ge(rank_sem, t.n * 2 + 1)
                V.reduce_sum(small3[:, t.s4, 0:B], keyT[:, t.h], AX).then_inc(rank_sem, 1)
                yield
                dve.wait_ge(rank_sem, t.n * 2 + 2)
                if t.late(2):
                    dve.wait_ge(qs["moved"], t.n - 1)
                tt(perm[:, t.h], iota_n[:, :].unsqueeze(1).to_broadcast([P, B, P]),
                   small3[:, t.s4, 0:B].unsqueeze(2).to_broadcast([P, B, P]), ALU.is_equal).then_inc(qs["perm"], 1)

            def sort_fields(t):
                dve.wait_ge(qs["moved"], t.n + 1)
                f = ps[:, 5, t.h * 64:t.h * 64 + 4 * B].rearrange("p (j c) -> p j c", j=B)
                for dst, c in ((idx1, 0), (dl, 1), (et, 2), (idx5, 3)):
                    V.tensor_scalar(dst[:, bass.ds(t.k * B, B)], f[:, :, c], 0.0, None, ALU.add).then_inc(qs["fields"], 1)

            def acc_gine(t):
                dve.wait_ge(qg["sums"], t.n + 1)
                yield from accumulate(qg, t, into(XL, D), lambda j: ps[:, 2 + t.h, j * P:(j + 1) * P])

            def add_gine(t):
                dve.wait_ge(qg.gath[t.s4], t.u * (16 * B) + 16 * B)
                dve.wait_ge(qg["edge"], t.n + 1)
                if t.late(2):
                    dve.wait_ge(qg["relu"], t.n - 1)
                tt(mraw[:, t.h], ps[:, t.h, :].rearrange("p (j d) -> p j d", j=B), ring[:, t.s4, :, 0:D], ALU.add).then_inc(qg["added"], 1)

            for l in range(3):
                join.to(f"weights{l}")
                one = onehots(qg["onehot"], qg["sums"], oh)
                if l == 0:
                    run(dve, [(3, sort_fields), (0, sort_keys), (10, acc_gine), (7, add_gine), (1, sort_places), (7, one)], l)
                else:
                    run(dve, [(3, acc_gine), (0, one), (1, add_gine)], l)
                dve.wait_ge(qg["acc"], NB * B * (l + 1))
                join.to(f"out{l}")
                norm(T3[4], XL, gb=True)
                if l < 2:
                    ch(tt(T3[0], XL, per_feature(bc[:, 2, :]), ALU.add))
                else:
                    ch(tt(X[:, :, :], X[:, :, :], XL, ALU.add))
                    norm(X[:, :, :], H[:, :, :], relu=True)
                    ch(V.memset(aren[:, 2 * NPAD:4 * NPAD], 0.0))
                join.to(f"norm{l}")

            join.to("rel_T")
            dve.wait_ge(relv_ps, 1)
            ch(V.tensor_copy(wt[:, NREL * D:NREL * D + 2 * NREL], ps[:, 4, 0:2 * NREL]))
            ch(V.memset(MX[:, :, :], -BIG))
            join.to("rel_table")

            def types(o, t):
                return tt(o, iota_n[:, 0:NREL].unsqueeze(1).to_broadcast([P, B, NREL]),
                          et[:, bass.ds(t.k * B, B)].unsqueeze(2).to_broadcast([P, B, NREL]), ALU.is_equal)

            ch_scan, ch_acc = Steps(dve, qm["ch_scan"], 4), Steps(dve, qm["ch_acc"], 2)

            def scan_max(n):
                def body(t):
                    ch_scan.start(t.n)
                    rows = B * n
                    z, key = tz[0:rows, t.h, 0:P], tz[0:rows, t.h, P:2 * P]
                    reset, f, start = sf[0:rows, t.h, 0:P], sf[0:rows, t.h, P:2 * P], ne[0:rows, t.h, :]
                    dve.wait_ge(qm["rows_sb"], t.n + 1)
                    if t.late(2):
                        dve.wait_ge(qm["back"], t.n - 1)
                    ch_scan.step(tt(start[:, 1:P], key[:, 1:P], key[:, 0:P - 1], ALU.not_equal))
                    yield
                    ch_scan.done()
                    ch_scan.step(V.tensor_scalar(reset, start[:, 0:P], -4 * BIG, None, ALU.mult))
                    yield
                    ch_scan.done()
                    ch_scan.step(V.tensor_tensor_scan(f, reset, z, 0.0, ALU.add, ALU.max))
                    yield
                    ch_scan.done()
                    ch_scan.step(tt(f, f, start[:, 1:P + 1], ALU.mult))
                    yield
                    ch_scan.done()
                    dve.sem_inc(qm["scanned"], 1)
                return body

            def acc_max(n, per_type):
                def body(t):
                    ch_acc.start(t.n)
                    dve.wait_ge(qm["sums"], t.n + 1)
                    w = 2 * NREL if per_type else n + 1
                    got = ps[:, 7, t.h * 64:t.h * 64 + B * w].rearrange("p (j c) -> p j c", j=B)
                    m = NREL if per_type else 1
                    miss = small4[:, t.s4, 0:B * m].rearrange("p (j c) -> p j c", j=B)
                    cand = small4[:, t.s4, 24:24 + B * n].rearrange("p (j c) -> p j c", j=B)
                    ch_acc.step(V.tensor_scalar(miss, got[:, :, n:n + m], BIG, -BIG, ALU.mult, ALU.add))
                    yield
                    ch_acc.done()
                    ch_acc.step(tt(cand, got[:, :, 0:n], miss if per_type else miss.to_broadcast([P, B, n]), ALU.add))
                    yield
                    ch_acc.done()
                    yield from accumulate(qm, t, into(MX, n), lambda j: cand[:, j, :], ALU.max)
                return body

            ch_rel, ch_pick = Steps(dve, qm["ch_score"], 3), Steps(dve, types_set, 1)

            def rel_score(t):
                ch_rel.start(t.n)
                dve.wait_ge(qm.gath[t.s4], t.u * (16 * B) + 16 * B)
                if t.late(4):
                    dve.wait_ge(qm["rows"], t.n - 3)
                sk = ring[:, t.s4, :, D]
                ch_rel.step(V.tensor_scalar(small3[:, t.s4, 0:B], sk, 0.0, None, ALU.add))
                yield
                ch_rel.done()
                ch_rel.step(V.tensor_scalar(SK[:, bass.ds(t.k * B, B)], sk, 0.0, None, ALU.add))
                yield
                ch_rel.done()
                ch_rel.step(V.scalar_tensor_tensor(small3[:, t.s4, 32:32 + B], dl[:, bass.ds(t.k * B, B)], 8.0,
                                              et[:, bass.ds(t.k * B, B)], ALU.mult, ALU.add))
                yield
                ch_rel.done()
                dve.sem_inc(qm["scores"], 1)

            def rel_pick(t):
                ch_pick.start(t.n)
                R = small2[:, t.s4, 0:B * NREL].rearrange("p (j r) -> p j r", j=B)
                ch_pick.step(types(R, t))
                yield
                ch_pick.done()
                dve.wait_ge(qm["back"], t.n + 1)
                if t.late(4):
                    dve.wait_ge(qm["sums"], t.n - 3)
                for c in range(2):
                    src = ps[:, 6, t.h * 128 + c * 32:t.h * 128 + c * 32 + B].unsqueeze(2).to_broadcast([P, B, NREL])
                    ins = tt(gm[:, t.s4, :, c * NREL:(c + 1) * NREL], R, src, ALU.mult)
                ins.then_inc(qm["picked"], 1)

            run(dve, [(9, acc_max(NREL, True)), (7, rel_pick), (2, rel_score), (5, scan_max(1)), (5, onehots(qm["onehot"], qm["sums"], oh))])
            dve.wait_ge(qm["acc"], NB * B)
            mxv, c1m = MX[:, :, 0:NREL], C1[:, :, NREL:2 * NREL]
            ch(tt(mxv, mxv, C1[:, :, 0:NREL], ALU.add))
            ch(V.scalar_tensor_tensor(c1m, mxv, 0.2, mxv, ALU.mult, ALU.max))
            ch(V.memset(DEN, 0.0))
            join.to("rel_max")

            ch_d = Steps(dve, qd["chain"], 7)

            def rel_logit(t):
                ch_d.start(t.n)
                w = B * NREL
                R = small[:, t.s4, 0:w].rearrange("p (j r) -> p j r", j=B)
                ch_d.step(types(R, t))
                yield
                ch_d.done()
                dve.wait_ge(qd["node"], t.n + 1)
                s, m = small3[:, t.s4, 0:2 * B:2], small3[:, t.s4, 1:2 * B:2]
                pick = small2[:, t.s4, 0:2 * w].rearrange("p (j c r) -> p j c r", j=B, c=2)
                nd = ps[:, 2 + t.h, 0:2 * w].rearrange("p (j c r) -> p j c r", j=B, c=2)
                ch_d.step(tt(pick, nd, R.unsqueeze(2).to_broadcast([P, B, 2, NREL]), ALU.mult))
                yield
                ch_d.done()
                ch_d.step(V.reduce_sum(small3[:, t.s4, 0:2 * B].rearrange("p (j c) -> p j c", j=B), pick, AX))
                yield
                ch_d.done()
                ch_d.step(tt(s, s, SK[:, bass.ds(t.k * B, B)], ALU.add))
                yield
                ch_d.done()
                ch_d.step(V.scalar_tensor_tensor(s, s, 0.2, s, ALU.mult, ALU.max))
                yield
                ch_d.done()
                ch_d.step(tt(s, s, m, ALU.subtract))
                yield
                ch_d.done()
                ch_d.step(V.tensor_scalar(s, s, 0.0, None, ALU.min))
                yield
                ch_d.done()
                dve.sem_inc(qd["logits"], 1)

            ch_w = Steps(dve, qd["chain2"], 2)

            def rel_weight(t):
                ch_w.start(t.n)
                R = small[:, t.s4, 0:B * NREL].rearrange("p (j r) -> p j r", j=B)
                p = small3[:, t.s4, 2 * B:3 * B]
                dve.wait_ge(qd["exp"], t.n + 1)
                ch_w.step(V.tensor_scalar(PW[:, bass.ds(t.k * B, B)], p, 0.0, None, ALU.add))
                yield
                ch_w.done()
                if t.late(4):
                    dve.wait_ge(qd["sums"], t.n - 3)
                ch_w.step(tt(gm[:, t.s4, :, 0:NREL], R, p.unsqueeze(2).to_broadcast([P, B, NREL]), ALU.mult))
                yield
                ch_w.done()
                dve.sem_inc(qd["weights"], 1)

            def acc_den(t):
                dve.wait_ge(qd["sums"], t.n + 1)
                yield from accumulate(qd, t, into(DEN, NREL), lambda j: ps[:, 4 + t.h, j * NREL:(j + 1) * NREL])

            run(dve, [(8, acc_den), (6, rel_weight), (4, rel_logit), (4, onehots(qd["onehot"], qd["sums"], oh)),
                      (0, onehots(qd["onehot_t"], qd["turned"], ohx))])
            dve.wait_ge(qd["acc"], NB * B)
            ch(V.tensor_scalar(DEN, DEN, 1e-10, None, ALU.add))
            ch(V.reciprocal(C1[:, :, 0:NREL], DEN))
            ch(V.memset(AG[:, :], 0.0))
            join.to("rel_den")

            ch_r = Steps(dve, qr["chain"], 4)

            def rel_message(t):
                ch_r.start(t.n)
                R = small[:, t.s4, 0:B * NREL].rearrange("p (j r) -> p j r", j=B)
                pick = small2[:, t.s4, 0:B * NREL].rearrange("p (j r) -> p j r", j=B)
                w = small3[:, t.s4, 0:B]
                ch_r.step(types(R, t))
                yield
                ch_r.done()
                dve.wait_ge(qr["node"], t.n + 1)
                ch_r.step(tt(pick, ps[:, 2 + t.h, 0:B * NREL].rearrange("p (j r) -> p j r", j=B), R, ALU.mult))
                yield
                ch_r.done()
                ch_r.step(V.reduce_sum(w, pick, AX))
                yield
                ch_r.done()
                ch_r.step(tt(w, w, PW[:, bass.ds(t.k * B, B)], ALU.mult))
                yield
                ch_r.done()
                dve.wait_ge(qr.gath[t.s4], t.u * (16 * B) + 16 * B)
                if t.late(4):
                    dve.wait_ge(qr["sums"], t.n - 3)
                tt(msg[:, t.s4, :, 0:D], ring[:, t.s4, :, 0:D], w.unsqueeze(2).to_broadcast([P, B, D]), ALU.mult).then_inc(qr["messages"], 1)

            def acc_pair(q, agg, w):
                def body(t):
                    dve.wait_ge(q["sums"], t.n + 1)
                    yield from accumulate(q, t, into(agg, w), lambda j: ps[:, 4 + 2 * t.h + j // 2, (j % 2) * 256:(j % 2) * 256 + w])
                return body

            run(dve, [(4, acc_pair(qr, agg2, D)), (2, rel_message), (0, onehots(qr["onehot"], qr["sums"], oh))])
            dve.wait_ge(qr["acc"], NB * B)
            hp, neg = agg2[:, :, 0:D], T3[0]
            ch(V.tensor_scalar(neg, hp, 0.0, None, ALU.min))
            dve.sem_inc(elu_in, 1)
            ch(V.tensor_scalar(hp, hp, 0.0, -1.0, ALU.max, ALU.add))
            ch(tt(X[:, :, :], X[:, :, :], hp, ALU.add))
            dve.wait_ge(elu_exp, 1)
            ch(tt(X[:, :, :], X[:, :, :], neg, ALU.add))
            norm(X[:, :, :], H[:, :, :], relu=True)
            join.to("rel_out")

            ch(V.memset(wt[:, 0:WK_o + NTYPE * D], 0.0))
            ch(V.memset(WE, 0.0))
            ch(V.memset(ntype_i, 0))
            ch(V.memset(MX[:, :, :], -BIG))
            join.to("tr_weights")
            ch(V.tensor_scalar(muv, muv, float(HD) ** -0.5, None, ALU.mult))
            ch(V.tensor_copy(ntype_f, ntype_i))
            for t, o in ((0, T3[3]), (1, T3[4]), (2, XL)):
                ch(V.tensor_scalar(stat[:, t, 0:NBLK], ntype_f, float(t), None, ALU.is_equal))
                ch(tt(o, H[:, :, :], per_block(stat[:, t, 0:NBLK]), ALU.mult))
            join.to("tr_masked")
            join.to("tr_qv")
            for b in range(NBLK):
                for part, r0, nr in ((0, 0, 4), (1, 4, 1)):
                    dve.wait_ge(kw_ps, 2 * b + part + 1)
                    if b >= 2:
                        dve.wait_ge(keys_out[b % 2], 16 * (b // 2))
                    for r in range(r0, r0 + nr):
                        ins = tt(kwb[:, b % 2, r * D:(r + 1) * D].rearrange("p (h d) -> p h d", h=NHEAD),
                                 ps[:, 4 + 2 * (b % 2) + part, (r - r0) * D:(r - r0 + 1) * D].rearrange("p (h d) -> p h d", h=NHEAD),
                                 muv.rearrange("p (h r) -> p h r", h=NHEAD)[:, :, r:r + 1].to_broadcast([P, NHEAD, HD]), ALU.mult)
                    ins.then_inc(vals_rdy, 1)
            dve.wait_ge(vals_rdy, 2 * NBLK)
            join.to("tr_values")
            ch_tr = Steps(dve, trs_sem, 4)

            def tr_score(t):
                ch_tr.start(t.k)
                s = small3[:, t.s4, 0:B * NHEAD]
                if t.late(4):
                    dve.wait_ge(qm["rows"], t.n - 3)
                ch_tr.step(V.tensor_scalar(small3[:, t.s4, 32:64].rearrange("p (j g) -> p j g", j=B),
                                      dl[:, bass.ds(t.k * B, B)].unsqueeze(2).to_broadcast([P, B, NHEAD]), 0.0, None, ALU.add))
                yield
                ch_tr.done()
                dve.wait_ge(qm.gath[t.s4], t.u * (16 * B) + 16 * B)
                dve.wait_ge(qm["node"], t.k + 1)
                ch_tr.step(tt(mraw[:, t.h], ps[:, 2 + t.h, :].rearrange("p (j d) -> p j d", j=B), ring[:, t.s4, :, 0:D], ALU.mult))
                yield
                ch_tr.done()
                ch_tr.step(V.reduce_sum(s.rearrange("p (g a) -> p g a", a=1), mraw[:, t.h].rearrange("p j (g d) -> p (j g) d", d=HD), AX))
                yield
                ch_tr.done()
                dve.sem_inc(qm["scores"], 1)
                ch_tr.step(V.tensor_scalar(score[:, bass.ds(t.k * (B * NHEAD), B * NHEAD)], s, 0.0, None, ALU.add))
                yield
                ch_tr.done()

            run(dve, [(11, acc_max(NHEAD, False)), (4, tr_score), (7, scan_max(NHEAD)), (7, onehots(qm["onehot"], qm["sums"], oh)),
                      (0, onehots(onehot_tr, qm["turned"], ohx, lambda t: t.k))], 1)
            dve.wait_ge(qm["acc"], 2 * NB * B)
            join.to("trA")
            ch(V.memset(AG[:, :], 0.0))
            join.to("tr_zero")

            def tr_logit(t):
                dve.wait_ge(qt["node"], t.n + 1)
                if t.late(4):
                    dve.wait_ge(qt["exp"], t.n - 3)
                tt(small3[:, t.s4, 0:B * NHEAD], score[:, bass.ds(t.k * (B * NHEAD), B * NHEAD)],
                   ps[:, 2 + t.h, 0:B * NHEAD], ALU.subtract).then_inc(qt["logits"], 1)

            def tr_message(t):
                dve.wait_ge(qt["exp"], t.n + 1)
                dve.wait_ge(qt.gath[t.s4], t.u * (16 * B) + 16 * B)
                for j in range(B):
                    ins = tt(msg[:, t.s4, j, 0:D].rearrange("p (g d) -> p g d", g=NHEAD),
                             ring[:, t.s4, j, 0:D].rearrange("p (g d) -> p g d", g=NHEAD),
                             msg[:, t.s4, j, D:W2N].unsqueeze(2).to_broadcast([P, NHEAD, HD]), ALU.mult)
                ins.then_inc(qt["messages"], 1)

            run(dve, [(5, acc_pair(qt, agg2, W2N)), (3, tr_message), (2, tr_logit), (0, onehots(qt["onehot"], qt["sums"], oh))])
            dve.wait_ge(qt["acc"], NB * B)
            join.to("trB")
            den = agg2[:, :, D:W2N]
            rden = T[4][:, 0:NBLK * NHEAD].rearrange("p (b g) -> p b g", b=NBLK)
            ch(V.tensor_scalar(rden, den, 1e-10, None, ALU.add))
            ch(V.reciprocal(rden, rden))
            for g in range(NHEAD):
                s = slice(g * HD, (g + 1) * HD)
                ch(tt(T3[0][:, :, s], agg2[:, :, s], rden[:, :, g:g + 1].to_broadcast([P, NBLK, HD]), ALU.mult))
            join.to("tr_mix")
            ch(tt(T3[2], T3[3], H[:, :, :], ALU.add))
            norm(T3[2], T3[0], gb=True)
            join.to("tr_norm1")
            join.to("tr_ff")
            ch(tt(T3[3], T3[3], T3[0], ALU.add))
            norm(T3[3], T3[1], gb=True)
            ch(tt(X[:, :, :], X[:, :, :], T3[1], ALU.add))
            norm(X[:, :, :], H[:, :, :], relu=True)
            ch(V.memset(AG[:, :], 0.0))
            ch(V.memset(msg[:, :, :, D:D + 1], 1.0))
            ch(V.memset(wt[:, 0:D], 0.0))
            ch(V.memset(ear[:, :, :], 0.0))
            join.to("tr_out")

            join.to("mp_T")
            for g in range((NBLK + 3) // 4):
                n = min(4, NBLK - 4 * g)
                dve.wait_ge(nt_ps, g + 1)
                tt(T3[2][:, 4 * g:4 * g + n, :], ps[:, 4 + g % 2, 0:n * P].rearrange("p (b d) -> p b d", b=n),
                   bc[:, 2, :].unsqueeze(1).to_broadcast([P, n, D]), ALU.add).then_inc(nt_free, 1)
            dve.wait_ge(nt_free, (NBLK + 3) // 4)
            join.to("mp_table")

            def mp_add(t):
                dve.wait_ge(qp.gath[t.s4], t.u * (16 * B) + 16 * B)
                dve.wait_ge(qp["node"], t.n + 1)
                if t.late(2):
                    dve.wait_ge(qp["relu"], t.n - 1)
                tt(mraw[:, t.h], ps[:, 2 + t.h, :].rearrange("p (j d) -> p j d", j=B), ring[:, t.s4, :, 0:D], ALU.add).then_inc(qp["added"], 1)

            run(dve, [(4, acc_pair(qp, agg3, D + 1)), (2, mp_add), (0, onehots(qp["onehot"], qp["sums"], oh))])
            dve.wait_ge(qp["acc"], NB * B)
            join.to("mp_upd")
            ch(tt(T3[3], T3[2], H[:, :, :], ALU.add))
            norm(T3[3], T3[0], gb=True)
            ch(tt(X[:, :, :], X[:, :, :], T3[0], ALU.add))
            join.to("mp_out")

        @block.scalar
        def _(act):
            join = Join(act)
            A = nc.scalar
            pn = [0]
            norms = [0]

            def evac(dst, func, bias=0.0, n=1, width=None):
                act.wait_ge(pn_full, pn[0] + 1)
                src = ps[:, 2 * (pn[0] % 2), 0:width]
                A.activation(dst, src, func, bias=bias).then_inc(pn_free, 1)
                pn[0] += 1

            def turned(dst):
                for g in range((NBLK + 3) // 4):
                    n = min(4, NBLK - 4 * g) * P
                    evac(dst[:, g * 512:g * 512 + n], ACT.Copy, width=n)
                act.wait_ge(pn_free, pn[0])

            def product(dst, func, bias):
                for g in range(NG):
                    evac(dst[:, g * G:(g + 1) * G], func, bias, width=G)
                act.wait_ge(pn_free, pn[0])

            def root():
                norms[0] += 1
                act.wait_ge(ln_var, norms[0])
                A.activation(stat[:, 2, 0:NBLK], stat[:, 1, 0:NBLK], ACT.Sqrt).then_inc(ln_std, 1)

            join.to("slots")
            root()

            def stage_indices(q, idx, first=False):
                def body(t):
                    if t.late(4):
                        act.wait_ge(q.gath[t.s4], t.u * (16 * B))
                    if first:
                        act.wait_ge(qs["fields"], t.n * 4 + 4)
                    act.sem_inc(act_go, 1)
                    A.copy(idxr[:, t.s4, :], idx[:, bass.ds(t.k * B, B)]).then_inc(q["index"], 1)
                return body

            def relu(q):
                def body(t):
                    act.wait_ge(q["added"], t.n + 1)
                    if t.late(4):
                        act.wait_ge(q["sums"], t.n - 3)
                    A.activation(msg[:, t.s4, :, 0:D], mraw[:, t.h], ACT.Relu).then_inc(q["relu"], 1)
                return body

            def attrs_out(t):
                act.wait_ge(qs["moved"], t.n + 1)
                if t.late(2):
                    act.wait_ge(rout[t.h], t.i * 16)
                A.activation(eato[:, t.h, :], ps[0:EAB, 4, :], ACT.Copy).then_inc(qs["attr_sb"], 1)
                act.wait_ge(qs["attr_sb"], t.n + 1)
                act.dma_start(eat[bass.ds(t.k, 1), :, :].rearrange("a p c -> p (a c)"), eato[:, t.h, :]).then_inc(rout[t.h], 16)

            for l in range(3):
                join.to(f"weights{l}")
                if l == 0:
                    run(act, [(3, attrs_out), (4, stage_indices(qg, idx1, True)), (8, relu(qg))], l)
                    for h in range(2):
                        act.wait_ge(rout[h], 16 * (NB // 2))
                else:
                    run(act, [(0, stage_indices(qg, idx1)), (2, relu(qg))], l)
                join.to(f"gine{l}")
                turned(T[1])
                join.to(f"sumT{l}")
                product(T[2], ACT.Relu, col[:, 0:1])
                join.to(f"hiddenT{l}")
                product(T[3], ACT.Relu, col[:, 1:2])
                join.to(f"outT{l}")
                turned(T[4])
                join.to(f"out{l}")
                root()
                if l == 2:
                    root()
            join.to("rel_weights")
            turned(T[0])
            join.to("rel_vectors")
            for b in range(NBLK):
                rows = T[2 + b % 2][:, 0:NREL * T1W].rearrange("p (r w) -> p r w", r=NREL)
                if b >= 2:
                    act.wait_ge(rows_out[b % 2], 16 * (b // 2))
                act.wait_ge(pn_full, pn[0] + 1)
                s = 2 * (pn[0] % 2)
                A.activation(rows[:, 0:4, 0:D], ps[:, s, :].rearrange("p (r d) -> p r d", r=4), ACT.Copy).then_inc(rows_rdy, 1)
                A.activation(rows[:, 4, 0:D], ps[:, s + 1, 0:D], ACT.Copy)
                A.activation(rows[:, :, D], ps[:, s + 1, D:D + NREL], ACT.Copy).then_inc(rows_rdy, 1)
                A.activation(C1[:, b, 0:NREL], ps[:, s + 1, D + NREL:D + 2 * NREL], ACT.Copy).then_inc(pn_free, 1)
                pn[0] += 1
            act.wait_ge(pn_free, pn[0])
            join.to("rel_table")

            def onehotT(q, count):
                def body(t):
                    n = count(t)
                    act.wait_ge(q["turned"], n + 1)
                    if t.has(2):
                        act.wait_ge(q["node"], n - 1)
                    A.activation(ohT[:, t.h], ps[:, t.h, :].rearrange("p (j d) -> p j d", j=B), ACT.Copy).then_inc(q["onehotT"], 1)
                return body

            def rows_copied(n):
                def body(t):
                    act.wait_ge(qm["rows"], t.n + 1)
                    if t.late(2):
                        act.wait_ge(qm["scanned"], t.n - 1)
                    A.activation(tz[0:B * n, t.h, :], ps[0:B * n, 4 + t.h, 0:2 * P], ACT.Copy).then_inc(qm["rows_sb"], 1)
                return body

            run(act, [(0, stage_indices(qm, idx5)), (4, rows_copied(1))])
            join.to("rel_max")

            def rel_exp(t):
                act.wait_ge(qd["logits"], t.n + 1)
                A.activation(small3[:, t.s4, 2 * B:3 * B], small3[:, t.s4, 0:2 * B:2], ACT.Exp).then_inc(qd["exp"], 1)

            run(act, [(2, onehotT(qd, lambda t: t.n)), (5, rel_exp)])
            join.to("rel_den")
            run(act, [(0, stage_indices(qr, idx5)), (0, onehotT(qr, lambda t: t.n))])
            act.wait_ge(elu_in, 1)
            A.activation(T3[0], T3[0], ACT.Exp).then_inc(elu_exp, 1)
            root()
            join.to("tr_masked")
            turned(T[0])
            turned(T[1])
            turned(T[2])
            join.to("tr_T")
            product(T[3], ACT.Copy, 0.0)
            join.to("tr_keysT")
            for b in range(NBLK):
                act.wait_ge(pn_full, pn[0] + 1)
                s = 2 * (pn[0] % 2)
                A.activation(Qn[:, b, :], ps[:, s, 0:D], ACT.Copy)
                A.activation(T3[4][:, b, :], ps[:, s, D:2 * D], ACT.Copy).then_inc(pn_free, 1)
                pn[0] += 1
            act.wait_ge(pn_free, pn[0])
            join.to("tr_values")

            def picked(t):
                act.wait_ge(qm["back"], t.n + 1)
                if t.late(4):
                    act.wait_ge(qm["sums"], t.n - 3)
                o = 128 * t.h
                A.activation(gm[:, t.s4, :, 0:NHEAD], ps[:, 6, o:o + B * NHEAD].rearrange("p (j g) -> p j g", j=B), ACT.Copy)
                A.activation(gm[:, t.s4, :, NHEAD:NHEAD + 1], ps[:, 6, o + 32:o + 32 + B * NHEAD].rearrange("p (j g) -> p j g", j=B)[:, :, 0:1],
                             ACT.Copy).then_inc(qm["picked"], 1)

            run(act, [(1, stage_indices(qm, idx5)), (6, rows_copied(NHEAD)), (9, picked), (2, onehotT(qm, lambda t: t.k))], 1)
            join.to("tr_zero")

            def tr_exp(t):
                act.wait_ge(qt["logits"], t.n + 1)
                if t.late(4):
                    act.wait_ge(qt["sums"], t.n - 3)
                A.activation(msg[:, t.s4, :, D:W2N], small3[:, t.s4, 0:B * NHEAD].rearrange("p (j g) -> p j g", j=B), ACT.Exp).then_inc(qt["exp"], 1)

            run(act, [(0, stage_indices(qt, idx1)), (2, tr_exp), (0, onehotT(qt, lambda t: t.n))])
            join.to("tr_mean")
            turned(T[1])
            join.to("tr_meanT")
            product(T[2], ACT.Identity, col[:, 0:1])
            join.to("tr_mixT")
            turned(T[3])
            join.to("tr_mix")
            root()
            join.to("tr_norm1")
            turned(T[1])
            join.to("tr_norm1T")
            hid = [T[2], T[3], T[4], AG[:, 0:NPAD]]
            for c in range(4):
                product(hid[c], ACT.Gelu, col[:, 1 + c:2 + c])
            join.to("tr_hiddenT")
            product(T[1], ACT.Identity, col[:, 5:6])
            join.to("tr_ffT")
            turned(T[3])
            join.to("tr_ff")
            root()
            root()
            join.to("mp_weights")
            turned(T[0])
            join.to("mp_T")
            turned(T[1])
            join.to("mp_table")
            run(act, [(0, stage_indices(qp, idx1)), (2, relu(qp)), (0, onehotT(qp, lambda t: t.n))])
            join.to("mp")
            turned(T[3])
            for g in range((NBLK + 3) // 4):
                n = min(4, NBLK - 4 * g) * P
                act.wait_ge(pn_full, pn[0] + 1)
                A.activation(T[4][0:1, g * 512:g * 512 + n], ps[0:1, 2 * (pn[0] % 2), 0:n], ACT.Copy).then_inc(pn_free, 1)
                pn[0] += 1
            act.wait_ge(pn_free, pn[0])
            join.to("mp_sumT")
            product(T[0], ACT.Copy, 0.0)
            join.to("mp_msgT")
            product(T[1], ACT.Relu, col[:, 0:1])
            join.to("mp_updT")
            turned(T[2])
            join.to("mp_upd")
            root()
            join.to("mp_out")

        @block.tensor
        def _(pe):
            join = Join(pe)
            M = nc.tensor
            pn = [0]

            def group():
                if pn[0] >= 2:
                    pe.wait_ge(pn_free, pn[0] - 1)
                pn[0] += 1
                return 2 * ((pn[0] - 1) % 2)

            def turn(src, cols=None):
                for g in range((NBLK + 3) // 4):
                    s = group()
                    for j in range(min(4, NBLK - 4 * g)):
                        o = ps[:, s, j * P:(j + 1) * P] if cols is None else ps[0:1, s, j * P:(j + 1) * P]
                        ins = M.transpose(o, src(4 * g + j), ident[:, :])
                    ins.then_inc(pn_full, 1)

            def turn_all(t):
                turn(lambda b: t[:, b, :])

            def product(*terms):
                for g in range(NG):
                    s = group()
                    for n, (w, x) in enumerate(terms):
                        ins = M.matmul(ps[:, s, 0:G], w, x[:, g * G:(g + 1) * G], start=(n == 0), stop=(n == len(terms) - 1))
                    ins.then_inc(pn_full, 1)

            def turned_back(t):
                turn(lambda b: t[:, b * P:(b + 1) * P])

            pe.wait_ge(cst, 6)
            pe.wait_ge(cnt_rdy, 1)
            M.matmul(ps[0:EP, 0, 0:NBLK], tri[0:EP, 0:EP], cnt[0:EP], start=True, stop=True)
            M.matmul(ps[:, 1, 0:NBLK], ones[0:EP, :], cnt[0:EP], start=True, stop=True).then_inc(cnt_ps, 1)
            join.to("records")

            def sums(q, w, out_of, ready="relu", rhs=None, taken=None):
                def body(t):
                    pe.wait_ge(q["onehot"], t.n + 1)
                    pe.wait_ge(q[ready], t.n + 1)
                    if taken:
                        if t.late(1):
                            pe.wait_ge(q[taken], t.n * 2)
                    elif t.late(2):
                        pe.wait_ge(q["acc"], t.n * B - B)
                    for j in range(B):
                        x = rhs(t, j) if rhs else msg[:, t.s4, j, 0:w]
                        ins = M.matmul(out_of(t, j), oh[:, t.s4, j, :], x, start=True, stop=True)
                    ins.then_inc(q["sums"], 1)
                return body

            def edge_terms(t):
                pe.wait_ge(qg.ea[t.h], t.i * 16 + 16)
                if t.late(2):
                    pe.wait_ge(qg["added"], t.n - 1)
                for j in range(B):
                    ins = M.matmul(ps[:, t.h, j * P:(j + 1) * P], ear[0:EA, t.h, j * P:(j + 1) * P], wt[0:EA, 0:D],
                                   start=True, stop=True)
                ins.then_inc(qg["edge"], 1)

            def keys_spread(t):
                pe.wait_ge(qs["keys"], t.n + 1)
                if t.late(2):
                    pe.wait_ge(rank_sem, t.n * 2 - 3)
                for j in range(B):
                    ins = M.transpose(ps[:, 6 + t.h, j * P:(j + 1) * P], small2[:, t.s4, j:j + 1].to_broadcast([P, P]), ident[:, :])
                ins.then_inc(qs["spread"], 1)

            def moved(t):
                pe.wait_ge(qs["perm"], t.n + 1)
                if t.late(1):
                    pe.wait_ge(qs["attr_sb"], t.n)
                    pe.wait_ge(qs["fields"], t.n * 4)
                for j in range(B):
                    M.matmul(ps[0:EAB, 4, j * P:(j + 1) * P], recin[:, t.s4, j, 0:EAB], perm[:, t.h, j, :], start=True, stop=True)
                for j in range(B):
                    ins = M.matmul(ps[:, 5, t.h * 64 + 4 * j:t.h * 64 + 4 * j + 4], perm[:, t.h, j, :], recin[:, t.s4, j, EAB:REC],
                                   start=True, stop=True)
                ins.then_inc(qs["moved"], 1)

            seg_gine = sums(qg, D, lambda t, j: ps[:, 2 + t.h, j * P:(j + 1) * P])
            for l in range(3):
                join.to(f"weights{l}")
                if l == 0:
                    run(pe, [(9, seg_gine), (6, edge_terms), (2, moved), (0, keys_spread)], l)
                else:
                    run(pe, [(2, seg_gine), (0, edge_terms)], l)
                join.to(f"gine{l}")
                turn_all(XL)
                join.to(f"sumT{l}")
                product((wt[:, D:2 * D], T[1]))
                join.to(f"hiddenT{l}")
                product((wt[:, 2 * D:3 * D], T[2]))
                join.to(f"outT{l}")
                turned_back(T[3])
            join.to("rel_weights")
            turn_all(H)
            join.to("rel_T")
            for r in range(2 * NREL):
                c = 0 if r < NREL else 1
                ins = M.matmul(ps[:, 4, r:r + 1], T[1][:, r * D:(r + 1) * D], col[:, c:c + 1], start=True, stop=True)
            ins.then_inc(relv_ps, 1)
            join.to("rel_vectors")
            for b in range(NBLK):
                s = group()
                hb = T[0][:, b * P:(b + 1) * P]
                M.matmul(ps[:, s, :], hb, wt[:, 0:512], start=True, stop=True)
                M.matmul(ps[:, s + 1, 0:D + 2 * NREL], hb, wt[:, 512:NREL * D + 2 * NREL], start=True, stop=True).then_inc(pn_full, 1)
            join.to("rel_table")

            def turn_onehot(q, count, made="onehot", buf=oh):
                def body(t):
                    pe.wait_ge(q[made] if made else onehot_tr, count(t) + 1)
                    if t.has(2):
                        pe.wait_ge(q["onehotT"], count(t) - 1)
                    for j in range(B):
                        ins = M.transpose(ps[:, t.h, j * P:(j + 1) * P], buf[:, t.s4 % buf.shape[1], j, :], ident[:, :])
                    ins.then_inc(q["turned"], 1)
                return body

            def turn_scores(n):
                def body(t):
                    pe.wait_ge(qm["scores"], t.n + 1)
                    if t.late(2):
                        pe.wait_ge(qm["rows_sb"], t.n - 1)
                    M.transpose(ps[0:B * n, 4 + t.h, 0:P], small3[:, t.s4, 0:B * n], ident[:, :])
                    M.transpose(ps[0:B * n, 4 + t.h, P:2 * P], small3[:, t.s4, 32:32 + B * n], ident[:, :]).then_inc(qm["rows"], 1)
                return body

            def turn_maxima(n):
                def body(t):
                    pe.wait_ge(qm["scanned"], t.n + 1)
                    if t.late(1):
                        pe.wait_ge(qm["picked"], t.n)
                    pe.sem_inc(pe_go, 1)
                    o, rows = 128 * t.h, B * n
                    M.transpose(ps[:, 6, o:o + rows], sf[0:rows, t.h, P:2 * P], ident[0:rows, 0:rows])
                    M.transpose(ps[:, 6, o + 32:o + 32 + rows], ne[0:rows, t.h, 1:P + 1], ident[0:rows, 0:rows]).then_inc(qm["back"], 1)
                return body

            def node_rows(q, rhs, out_of, count, free):
                def body(t):
                    pe.wait_ge(q["onehotT"], count(t) + 1)
                    if t.has(2):
                        pe.wait_ge(q[free], t.n - 1)
                    blocks = blocks_of(pe, PE, t)
                    for j in range(B):
                        ins = M.matmul(out_of(t, j), ohT[:, t.h, j, :], rhs(blocks[j]), start=True, stop=True)
                    ins.then_inc(q["node"], 1)
                return body

            def rows_at(v, w):
                return lambda b: v[:, bass.ds(b, 1), 0:w].rearrange("p a w -> p (a w)")

            own = lambda t: t.n
            run(pe, [(8, sums(qm, 0, lambda t, j: ps[:, 7, t.h * 64 + 10 * j:t.h * 64 + 10 * j + 10], ready="picked", taken="ch_acc",
                              rhs=lambda t, j: gm[:, t.s4, j, 0:10])),
                     (3, turn_scores(1)), (6, turn_maxima(1))])
            join.to("rel_max")
            run(pe, [(7, sums(qd, 0, lambda t, j: ps[:, 4 + t.h, j * NREL:(j + 1) * NREL], ready="weights",
                              rhs=lambda t, j: gm[:, t.s4, j, 0:NREL])),
                     (3, node_rows(qd, rows_at(C1, 2 * NREL), lambda t, j: ps[:, 2 + t.h, j * 2 * NREL:(j + 1) * 2 * NREL], own, "logits")),
                     (1, turn_onehot(qd, own, "onehot_t", ohx))])
            join.to("rel_den")

            def pair(w):
                return lambda t, j: ps[:, 4 + 2 * t.h + j // 2, (j % 2) * 256:(j % 2) * 256 + w]

            run(pe, [(3, sums(qr, D, pair(D), ready="messages")),
                     (1, node_rows(qr, rows_at(C1, NREL), lambda t, j: ps[:, 2 + t.h, j * NREL:(j + 1) * NREL], own, "messages")),
                     (0, turn_onehot(qr, own))])
            join.to("tr_masked")
            turn_all(T3[3])
            turn_all(T3[4])
            turn_all(XL)
            join.to("tr_T")
            product(*[(WKb[:, t, :], T[t]) for t in range(NTYPE)])
            join.to("tr_keysT")
            for b in range(NBLK):
                s = group()
                for t in range(NTYPE):
                    ins = M.matmul(ps[:, s, 0:2 * D], T[t][:, b * P:(b + 1) * P], WQV[:, t, :], start=(t == 0), stop=(t == NTYPE - 1))
                ins.then_inc(pn_full, 1)
            join.to("tr_qv")
            for b in range(NBLK):
                kb, s = T[3][:, b * P:(b + 1) * P], 4 + 2 * (b % 2)
                if b >= 2:
                    pe.wait_ge(vals_rdy, 2 * (b - 1))
                M.matmul(ps[:, s, :], kb, WE[:, 0:512], start=True, stop=True).then_inc(kw_ps, 1)
                M.matmul(ps[:, s + 1, 0:D], kb, WE[:, 512:NREL * D], start=True, stop=True).then_inc(kw_ps, 1)
            join.to("tr_values")
            local = lambda t: t.k
            run(pe, [(10, sums(qm, 0, lambda t, j: ps[:, 7, t.h * 64 + 9 * j:t.h * 64 + 9 * j + 9], ready="picked", taken="ch_acc",
                              rhs=lambda t, j: gm[:, t.s4, j, 0:9])),
                     (3, node_rows(qm, rows_at(Qn, D), lambda t, j: ps[:, 2 + t.h, j * P:(j + 1) * P], local, "scores")),
                     (5, turn_scores(NHEAD)), (8, turn_maxima(NHEAD)), (1, turn_onehot(qm, local, None, ohx))], 1)
            join.to("tr_zero")
            run(pe, [(4, sums(qt, W2N, pair(W2N), ready="messages")),
                     (1, node_rows(qt, rows_at(MX, NHEAD), lambda t, j: ps[:, 2 + t.h, j * NHEAD:(j + 1) * NHEAD], own, "logits")),
                     (0, turn_onehot(qt, own))])
            join.to("tr_mean")
            turn_all(T3[0])
            join.to("tr_meanT")
            product((wt[:, 0:D], T[1]))
            join.to("tr_mixT")
            turned_back(T[2])
            join.to("tr_norm1")
            turn_all(T3[0])
            join.to("tr_norm1T")
            for c in range(4):
                product((wt[:, D + c * D:D + (c + 1) * D], T[1]))
            join.to("tr_hiddenT")
            hid = [T[2], T[3], T[4], AG[:, 0:NPAD]]
            product(*[(wt[:, D + FF + c * D:D + FF + (c + 1) * D], hid[c]) for c in range(4)])
            join.to("tr_ffT")
            turned_back(T[1])
            join.to("mp_weights")
            turn_all(H)
            join.to("mp_T")
            for g in range((NBLK + 3) // 4):
                s, n = group(), min(4, NBLK - 4 * g)
                for j in range(n):
                    hb = T[0][:, (4 * g + j) * P:(4 * g + j + 1) * P]
                    ins = M.matmul(ps[:, s, j * P:(j + 1) * P], hb, wt[:, D:2 * D], start=True, stop=True)
                ins.then_inc(pn_full, 1)
                if g >= 2:
                    pe.wait_ge(nt_free, g - 1)
                for j in range(n):
                    hb = T[0][:, (4 * g + j) * P:(4 * g + j + 1) * P]
                    ins = M.matmul(ps[:, 4 + g % 2, j * P:(j + 1) * P], hb, wt[:, 2 * D:3 * D], start=True, stop=True)
                ins.then_inc(nt_ps, 1)
            join.to("mp_table")

            def nd_mp(t):
                pe.wait_ge(qp["onehotT"], t.n + 1)
                pe.wait_ge(qp.ea[t.h], t.i * 16 + 16)
                if t.late(2):
                    pe.wait_ge(qp["added"], t.n - 1)
                blocks = blocks_of(pe, PE, t)
                for j in range(B):
                    o = ps[:, 2 + t.h, j * P:(j + 1) * P]
                    M.matmul(o, ear[:, t.h, j * P:(j + 1) * P], wt[:, 0:D], start=True, stop=False)
                    ins = M.matmul(o, ohT[:, t.h, j, :], rows_at(T3[2], D)(blocks[j]), start=False, stop=True)
                ins.then_inc(qp["node"], 1)

            run(pe, [(3, sums(qp, D + 1, pair(D + 1))), (1, nd_mp), (0, turn_onehot(qp, own))])
            join.to("mp")
            turn(lambda b: agg3[:, b, 0:D])
            turn(lambda b: agg3[:, b, D:D + 1], cols=1)
            join.to("mp_sumT")
            product((wt[:, 3 * D:4 * D], T[3]), (b2row[0:1, :], T[4][0:1]))
            join.to("mp_msgT")
            product((wt[:, 4 * D:5 * D], T[0]))
            join.to("mp_updT")
            turned_back(T[1])
            join.to("mp_out")


_INS = ["x", "src", "dst", "edge_attr_32", "edge_attr_64", "edge_type_5", "node_type_3",
        "L0_gnn_We", "L0_gnn_be", "L0_gnn_W1", "L0_gnn_b1", "L0_gnn_W2", "L0_gnn_b2", "L0_gnn_gamma", "L0_gnn_beta",
        "L1_gnn_WV", "L1_gnn_a_vec",
        "L2_gnn_W_Q", "L2_gnn_W_K", "L2_gnn_W_V", "L2_gnn_W_edge", "L2_gnn_mu", "L2_gnn_W_out", "L2_gnn_b_out",
        "L2_gnn_ln1_g", "L2_gnn_ln1_b", "L2_gnn_W1", "L2_gnn_b1", "L2_gnn_W2", "L2_gnn_b2", "L2_gnn_ln2_g", "L2_gnn_ln2_b",
        "L3_gnn_b1", "L3_gnn_b2", "L3_gnn_bu", "L3_gnn_gamma", "L3_gnn_beta"]
_TURNED = {"WKT": ("L1_gnn_WK", (0, 2, 1)), "WQT": ("L1_gnn_WQ", (0, 2, 1)), "W3T": ("L3_gnn_W1", (1, 0)),
           "W32T": ("L3_gnn_W2", (1, 0)), "WuT": ("L3_gnn_Wu", (1, 0))}


def kernel(**inputs):
    import concourse.bacc as _bacc
    from concourse.bass_utils import run_bass_kernel_spmd as _run

    nc = _bacc.Bacc("TRN2", target_bir_lowering=False, num_devices=1)
    arrays, args = {}, {}
    laid = {name: inputs[name] for name in _INS}
    laid.update({name: np.transpose(inputs[of], axes) for name, (of, axes) in _TURNED.items()})
    for name, v in laid.items():
        v = np.ascontiguousarray(v)
        arrays[f"in_{name}"] = v
        args[name] = nc.dram_tensor(f"in_{name}", v.shape, mybir.dt.from_np(v.dtype), kind="ExternalInput").ap()
    out = nc.dram_tensor("out_x", (N, D), F32, kind="ExternalOutput").ap()
    build(nc, args, out)
    r = _run(nc, [arrays], core_ids=[0])
    return r.results[0]["out_x"]
```
